# Optimizing a Trainium2 kernel written in Bass

```python
import numpy as np
import jax
import jax.numpy as jnp

def _softmax(x, axis=-1):
    return jax.nn.softmax(x, axis=axis)

def _gelu(x):
    return jax.nn.gelu(x, approximate=True)

def _silu(x):
    return jax.nn.silu(x)

def _sigmoid(x):
    return jax.nn.sigmoid(x)

def _layernorm(x, axis=-1, eps=1e-05):
    m = jnp.mean(x, axis=axis, keepdims=True)
    v = jnp.var(x, axis=axis, keepdims=True)
    return (x - m) / jnp.sqrt(v + eps)

def _scatter_add(tgt, idx, src, axis=0):
    return tgt.at[idx].add(src)

def _segment_sum(src, seg, n):
    return jax.ops.segment_sum(src, seg, n)
kernel_name = 'mk_xattn_ffn_d2_seqx_r8_b00b22'

def setup_inputs(seed: int=0):
    np.random.seed(seed)
    _w = jnp.asarray

    def _rec_inputs():
        import jax
        import jax.numpy as jnp
        _rk = jax.random.key(seed)
        x = 7.22e-05 + 1 * jax.random.normal(jax.random.fold_in(_rk, 1), (4, 512, 128), jnp.float32)
        _lenS = 512 - jax.random.randint(jax.random.fold_in(_rk, 7), (4,), 0, max(1, 512 // 4) + 1, jnp.int32)
        _lenS2 = 77 - jax.random.randint(jax.random.fold_in(_rk, 8), (4,), 0, max(1, 77 // 4) + 1, jnp.int32)
        _ctx_1024P = jax.random.normal(jax.random.fold_in(_rk, 11), (4, 16, 128), jnp.float32)
        _ctx_1024c = jax.random.dirichlet(jax.random.fold_in(_rk, 511), 0.3 * jnp.ones((16,), jnp.float32), (4, 77))
        _ctx_1024t = jnp.einsum('bsk,bkd->bsd', _ctx_1024c, _ctx_1024P)
        _ctx_1024t = _ctx_1024t * jax.lax.rsqrt(jnp.mean(jnp.square(_ctx_1024t)) + 1e-12) * 0.953939
        ctx_1024 = 4.13588e-05 + 0.999923 * (_ctx_1024t + 0.3 * jax.random.normal(jax.random.fold_in(_rk, 611), (4, 77, 128), jnp.float32))
        fside_Bx16xSxS2_0 = 0.000150688 + 1.00006 * jax.random.normal(jax.random.fold_in(_rk, 12), (4, 16, 512, 77), jnp.float32)
        fside_SxS2_0 = -2.64403e-05 + 0.100002 * jax.random.normal(jax.random.fold_in(_rk, 15), (512, 77), jnp.float32)
        _validS = jnp.arange(512)[None, :] < _lenS[:, None]
        _validS2 = jnp.arange(77)[None, :] < _lenS2[:, None]
        _causal = jnp.tril(jnp.ones((512, 512), dtype=bool))
        mask_BxSxS2_ik1 = jnp.where(jnp.broadcast_to(_validS2[:, None, :], (4, 512, 77)), 1, 0).astype(jnp.int32)
        mask_BxS2_bf0 = jnp.logical_not(jnp.ones((4, 77), dtype=bool))
        return (x, ctx_1024, fside_Bx16xSxS2_0, fside_SxS2_0, mask_BxSxS2_ik1, mask_BxS2_bf0)
    x, ctx_1024, fside_Bx16xSxS2_0, fside_SxS2_0, mask_BxSxS2_ik1, mask_BxS2_bf0 = _rec_inputs()

    def _L0_xattn_setup():
        import jax, jax.numpy as jnp
        import numpy as np
        import math
        H = 16
        D_MODEL = 128
        D_K = D_MODEL // H
        B, N = (16, 64)

        def _split_heads(x):
            b, n, _ = x.shape
            return x.reshape(b, n, H, D_K).transpose(0, 2, 1, 3)
        key = jax.random.key(seed)
        ks = jax.random.split(key, 14)
        s = 1.0 / math.sqrt(D_MODEL)
        inp = {'query': jax.random.normal(ks[0], (B, N, D_MODEL), jnp.float32), 'key': jax.random.normal(ks[1], (B, N, D_MODEL), jnp.float32), 'value': jax.random.normal(ks[2], (B, N, D_MODEL), jnp.float32), 'attention_bias': jax.random.normal(ks[3], (B, H, N, N), jnp.float32), 'mask': jax.random.randint(ks[4], (B, N, N), 0, 2, jnp.int32), 'Wq': jax.random.normal(ks[5], (D_MODEL, D_MODEL), jnp.float32) * s, 'bq': jnp.zeros((D_MODEL,), jnp.float32), 'Wk': jax.random.normal(ks[6], (D_MODEL, D_MODEL), jnp.float32) * s, 'bk': jnp.zeros((D_MODEL,), jnp.float32), 'Wv': jax.random.normal(ks[7], (D_MODEL, D_MODEL), jnp.float32) * s, 'bv': jnp.zeros((D_MODEL,), jnp.float32), 'Wo': jax.random.normal(ks[8], (D_MODEL, D_MODEL), jnp.float32) * s, 'bo': jnp.zeros((D_MODEL,), jnp.float32)}
        return inp
    _L0_xattn_all = _L0_xattn_setup()
    _L0_xattn_in = {k: v for k, v in _L0_xattn_all.items() if k in ('Wq', 'bq', 'Wk', 'bk', 'Wv', 'bv', 'Wo', 'bo')}
    del _L0_xattn_all

    def _L0_ffn_setup():
        import jax, jax.numpy as jnp
        import numpy as np
        NUM_EXPERTS = 8
        NUM_SELECTED = 2
        EXPERT_CAPACITY = 64
        NUM_GROUPS = 8

        def _routing(xg, w_router):
            G, T, H = xg.shape
            logits = jnp.einsum('gth,he->gte', xg, w_router)
            probs = jax.nn.softmax(logits, axis=-1)
            _gate, idx = jax.lax.top_k(probs, NUM_SELECTED)
            idx_kt = jnp.swapaxes(idx, 1, 2).reshape(G, -1)
            expert_mask = jax.nn.one_hot(idx_kt, NUM_EXPERTS, dtype=jnp.int32)
            priority = jnp.cumsum(expert_mask, axis=1) * expert_mask - 1
            priority = priority.reshape(G, NUM_SELECTED, T, NUM_EXPERTS)
            priority = jnp.swapaxes(priority, 1, 2).max(axis=2)
            dispatch = jax.nn.one_hot(priority, EXPERT_CAPACITY, dtype=xg.dtype)
            combine = probs[..., None] * dispatch
            return (dispatch, combine)
        key = jax.random.key(seed)
        k1, k2, k3, k4 = jax.random.split(key, 4)
        B, S, H, F = (8, 256, 128, 512)
        return {'x': jax.random.normal(k1, (B, S, H), jnp.float32), 'w_router': jax.random.normal(k2, (H, NUM_EXPERTS), jnp.float32) * 0.02, 'wi': jax.random.normal(k3, (NUM_EXPERTS, H, F), jnp.float32) * 0.02, 'wo': jax.random.normal(k4, (NUM_EXPERTS, F, H), jnp.float32) * 0.02}
    _L0_ffn_all = _L0_ffn_setup()
    _L0_ffn_in = {k: v for k, v in _L0_ffn_all.items() if k in ('w_router', 'wi', 'wo')}
    del _L0_ffn_all

    def _L1_xattn_setup():
        import jax, jax.numpy as jnp
        import numpy as np
        E = 128
        H = 16
        D = E // H
        key = jax.random.key(seed)
        ks = jax.random.split(key, 12)
        B, T, S = (2, 256, 256)
        inp = {'query': jax.random.normal(ks[0], (B, T, E), jnp.float32), 'key': jax.random.normal(ks[1], (B, S, E), jnp.float32), 'value': jax.random.normal(ks[2], (B, S, E), jnp.float32), 'spatial_bias': jax.random.normal(ks[3], (B, H, T, S), jnp.float32) * 0.1, 'directional_bias': jax.random.normal(ks[4], (B, H, T, S), jnp.float32) * 0.1, 'key_padding_mask': jnp.zeros((B, S), dtype=bool), 'attn_mask': jax.random.normal(ks[5], (T, S), jnp.float32) * 0.1, 'Wq': jax.random.normal(ks[6], (E, E), jnp.float32) / np.sqrt(E), 'bq': jnp.zeros((E,), jnp.float32), 'Wk': jax.random.normal(ks[7], (E, E), jnp.float32) / np.sqrt(E), 'bk': jnp.zeros((E,), jnp.float32), 'Wv': jax.random.normal(ks[8], (E, E), jnp.float32) / np.sqrt(E), 'bv': jnp.zeros((E,), jnp.float32), 'Wo': jax.random.normal(ks[9], (E, E), jnp.float32) / np.sqrt(E), 'bo': jnp.zeros((E,), jnp.float32)}
        return inp
    _L1_xattn_all = _L1_xattn_setup()
    _L1_xattn_in = {k: v for k, v in _L1_xattn_all.items() if k in ('Wq', 'bq', 'Wk', 'bk', 'Wv', 'bv', 'Wo', 'bo')}
    del _L1_xattn_all

    def _L1_ffn_setup():
        import jax, jax.numpy as jnp
        import numpy as np
        NUM_TRUE = 8
        NUM_NULL = 2
        NUM_EXPERTS = NUM_TRUE + NUM_NULL
        TOP_K = 2
        key = jax.random.key(seed)
        k0, k1, k2 = jax.random.split(key, 3)
        B, S, D = (4, 256, 128)
        inputs = jax.random.normal(k0, (B, S, D), dtype=jnp.float32)
        gate_w = jax.random.normal(k1, (NUM_EXPERTS, D), dtype=jnp.float32) * 0.02
        gate_b = jnp.zeros((NUM_EXPERTS,), dtype=jnp.float32)
        expert_w = jax.random.normal(k2, (NUM_TRUE, D, D), dtype=jnp.float32) * 0.02
        expert_b = jnp.zeros((NUM_TRUE, D), dtype=jnp.float32)
        return {'inputs': inputs, 'gate_w': gate_w, 'gate_b': gate_b, 'expert_w': expert_w, 'expert_b': expert_b}
    _L1_ffn_all = _L1_ffn_setup()
    _L1_ffn_in = {k: v for k, v in _L1_ffn_all.items() if k in ('gate_w', 'gate_b', 'expert_w', 'expert_b')}
    del _L1_ffn_all
    return {'x': x, 'ctx_1024': ctx_1024, 'fside_Bx16xSxS2_0': fside_Bx16xSxS2_0, 'fside_SxS2_0': fside_SxS2_0, 'mask_BxSxS2_ik1': mask_BxSxS2_ik1, 'mask_BxS2_bf0': mask_BxS2_bf0, 'L0_xattn_Wq': _L0_xattn_in['Wq'], 'L0_xattn_bq': _L0_xattn_in['bq'], 'L0_xattn_Wk': _L0_xattn_in['Wk'], 'L0_xattn_bk': _L0_xattn_in['bk'], 'L0_xattn_Wv': _L0_xattn_in['Wv'], 'L0_xattn_bv': _L0_xattn_in['bv'], 'L0_xattn_Wo': _L0_xattn_in['Wo'], 'L0_xattn_bo': _L0_xattn_in['bo'], 'L0_ffn_w_router': _L0_ffn_in['w_router'], 'L0_ffn_wi': _L0_ffn_in['wi'], 'L0_ffn_wo': _L0_ffn_in['wo'], 'L1_xattn_Wq': _L1_xattn_in['Wq'], 'L1_xattn_bq': _L1_xattn_in['bq'], 'L1_xattn_Wk': _L1_xattn_in['Wk'], 'L1_xattn_bk': _L1_xattn_in['bk'], 'L1_xattn_Wv': _L1_xattn_in['Wv'], 'L1_xattn_bv': _L1_xattn_in['bv'], 'L1_xattn_Wo': _L1_xattn_in['Wo'], 'L1_xattn_bo': _L1_xattn_in['bo'], 'L1_ffn_gate_w': _L1_ffn_in['gate_w'], 'L1_ffn_gate_b': _L1_ffn_in['gate_b'], 'L1_ffn_expert_w': _L1_ffn_in['expert_w'], 'L1_ffn_expert_b': _L1_ffn_in['expert_b']}

def reference(x, ctx_1024, fside_Bx16xSxS2_0, fside_SxS2_0, mask_BxSxS2_ik1, mask_BxS2_bf0, L0_xattn_Wq, L0_xattn_bq, L0_xattn_Wk, L0_xattn_bk, L0_xattn_Wv, L0_xattn_bv, L0_xattn_Wo, L0_xattn_bo, L0_ffn_w_router, L0_ffn_wi, L0_ffn_wo, L1_xattn_Wq, L1_xattn_bq, L1_xattn_Wk, L1_xattn_bk, L1_xattn_Wv, L1_xattn_bv, L1_xattn_Wo, L1_xattn_bo, L1_ffn_gate_w, L1_ffn_gate_b, L1_ffn_expert_w, L1_ffn_expert_b):
    import jax
    import jax.numpy as jnp

    def _L0_xattn_ref(query, key, value, attention_bias, mask, Wq, bq, Wk, bk, Wv, bv, Wo, bo):
        import jax, jax.numpy as jnp
        import numpy as np
        import math
        H = 16
        D_MODEL = 128
        D_K = D_MODEL // H
        B, N = (16, 64)

        def _split_heads(x):
            b, n, _ = x.shape
            return x.reshape(b, n, H, D_K).transpose(0, 2, 1, 3)
        q = _split_heads(query @ Wq.T + bq)
        k = _split_heads(key @ Wk.T + bk)
        v = _split_heads(value @ Wv.T + bv)
        scores = jnp.einsum('bhid,bhjd->bhij', q, k) / math.sqrt(D_K)
        scores = scores + attention_bias
        scores = jnp.where(mask[:, None, :, :] == 0, jnp.float32(-1000000000.0), scores)
        p = jax.nn.softmax(scores, axis=-1)
        x = jnp.einsum('bhij,bhjd->bhid', p, v)
        x = x.transpose(0, 2, 1, 3).reshape(query.shape[0], query.shape[1], D_MODEL)
        return x @ Wo.T + bo

    def _L0_ffn_ref(x, w_router, wi, wo):
        import jax, jax.numpy as jnp
        import numpy as np
        NUM_EXPERTS = 8
        NUM_SELECTED = 2
        EXPERT_CAPACITY = 64
        NUM_GROUPS = 8

        def _routing(xg, w_router):
            G, T, H = xg.shape
            logits = jnp.einsum('gth,he->gte', xg, w_router)
            probs = jax.nn.softmax(logits, axis=-1)
            _gate, idx = jax.lax.top_k(probs, NUM_SELECTED)
            idx_kt = jnp.swapaxes(idx, 1, 2).reshape(G, -1)
            expert_mask = jax.nn.one_hot(idx_kt, NUM_EXPERTS, dtype=jnp.int32)
            priority = jnp.cumsum(expert_mask, axis=1) * expert_mask - 1
            priority = priority.reshape(G, NUM_SELECTED, T, NUM_EXPERTS)
            priority = jnp.swapaxes(priority, 1, 2).max(axis=2)
            dispatch = jax.nn.one_hot(priority, EXPERT_CAPACITY, dtype=xg.dtype)
            combine = probs[..., None] * dispatch
            return (dispatch, combine)
        B, S, H = x.shape
        T = B * S // NUM_GROUPS
        xg = x.reshape(NUM_GROUPS, T, H)
        dispatch, combine = _routing(xg, w_router)
        expert_in = jnp.einsum('gth,gtec->gech', xg, dispatch)
        h = jax.nn.gelu(jnp.einsum('gech,ehf->gecf', expert_in, wi))
        expert_out = jnp.einsum('gecf,efh->gech', h, wo)
        out = jnp.einsum('gech,gtec->gth', expert_out, combine)
        return out.reshape(B, S, H)

    def _L1_xattn_ref(query, key, value, spatial_bias, directional_bias, key_padding_mask, attn_mask, Wq, bq, Wk, bk, Wv, bv, Wo, bo):
        import jax, jax.numpy as jnp
        import numpy as np
        E = 128
        H = 16
        D = E // H
        B, T, _ = query.shape
        S = key.shape[1]
        scale = D ** (-0.5)
        q = (query @ Wq.T + bq).reshape(B, T, H, D).transpose(0, 2, 1, 3)
        k = (key @ Wk.T + bk).reshape(B, S, H, D).transpose(0, 2, 1, 3)
        v = (value @ Wv.T + bv).reshape(B, S, H, D).transpose(0, 2, 1, 3)
        scores = jnp.einsum('bhtd,bhsd->bhts', q, k) * scale
        scores = scores + attn_mask[None, None, :, :]
        pad = key_padding_mask[:, None, None, :]
        scores = jnp.where(pad, -jnp.inf, scores)
        if T == S:
            scores = scores + spatial_bias + directional_bias
        probs = jax.nn.softmax(scores, axis=-1)
        out = jnp.einsum('bhts,bhsd->bhtd', probs, v)
        out = out.transpose(0, 2, 1, 3).reshape(B, T, E)
        return out @ Wo.T + bo

    def _L1_ffn_ref(inputs, gate_w, gate_b, expert_w, expert_b):
        import jax, jax.numpy as jnp
        import numpy as np
        NUM_TRUE = 8
        NUM_NULL = 2
        NUM_EXPERTS = NUM_TRUE + NUM_NULL
        TOP_K = 2
        D = inputs.shape[-1]
        x = inputs.reshape(-1, D)
        gate_logits = x @ gate_w.T + gate_b
        gate_probs = jax.nn.softmax(gate_logits, axis=-1)
        weights, selected = jax.lax.top_k(gate_probs, TOP_K)
        true_mask = selected < NUM_TRUE
        true_weights = weights * true_mask
        denom = true_weights.sum(axis=-1, keepdims=True)
        denom = jnp.where(denom > 0, denom, jnp.ones_like(denom))
        norm_w = (true_weights / denom).astype(x.dtype)
        one_hot = jax.nn.one_hot(selected, NUM_EXPERTS, dtype=norm_w.dtype)
        combine_w = jnp.einsum('tk,tke->te', norm_w, one_hot)[:, :NUM_TRUE]
        expert_out = jnp.einsum('td,edh->teh', x, expert_w) + expert_b[None, :, :]
        out = jnp.einsum('te,teh->th', combine_w, expert_out)
        return out.reshape(inputs.shape[:-1] + (out.shape[-1],))
    x = x + _L0_xattn_ref(_layernorm(x, axis=-1), ctx_1024, ctx_1024, fside_Bx16xSxS2_0, mask_BxSxS2_ik1, L0_xattn_Wq, L0_xattn_bq, L0_xattn_Wk, L0_xattn_bk, L0_xattn_Wv, L0_xattn_bv, L0_xattn_Wo, L0_xattn_bo)
    x = x + _L0_ffn_ref(_layernorm(x, axis=-1), L0_ffn_w_router, L0_ffn_wi, L0_ffn_wo)
    x = x + _L1_xattn_ref(_layernorm(x, axis=-1), ctx_1024, ctx_1024, fside_Bx16xSxS2_0, fside_Bx16xSxS2_0, mask_BxS2_bf0, fside_SxS2_0, L1_xattn_Wq, L1_xattn_bq, L1_xattn_Wk, L1_xattn_bk, L1_xattn_Wv, L1_xattn_bv, L1_xattn_Wo, L1_xattn_bo)
    x = x + _L1_ffn_ref(_layernorm(x, axis=-1), L1_ffn_gate_w, L1_ffn_gate_b, L1_ffn_expert_w, L1_ffn_expert_b)
    return x

_drawn_inputs = setup_inputs


def setup_inputs(seed=0):
    import zlib

    import numpy as np

    out = dict(_drawn_inputs(seed))
    spreads = {'L0_xattn_bq': (0.0, 0.1),
     'L0_xattn_bk': (0.0, 2.0),
     'L0_xattn_bv': (0.0, 0.1),
     'L0_xattn_bo': (0.0, 0.1),
     'L1_xattn_bq': (0.0, 0.1),
     'L1_xattn_bk': (0.0, 2.0),
     'L1_xattn_bv': (0.0, 0.1),
     'L1_xattn_bo': (0.0, 0.1),
     'L1_ffn_gate_b': (0.0, 0.1),
     'L1_ffn_expert_b': (0.0, 0.1)}
    factors = {'L0_ffn_w_router': 3.196, 'L0_ffn_wi': 3.318, 'L0_ffn_wo': 3.321, 'fside_SxS2_0': 3.035}
    for name, (base, spread) in spreads.items():
        noise = np.random.default_rng([zlib.crc32(name.encode()), seed]).standard_normal(out[name].shape)
        drawn = base * np.exp(spread * noise) if base else spread * noise
        out[name] = jnp.asarray(drawn.astype(out[name].dtype))
    for name, factor in factors.items():
        out[name] = (out[name] * factor).astype(out[name].dtype)
    return out
```

```python
from contextlib import ExitStack

import concourse.bass as bass
from concourse import mybir

F32 = mybir.dt.float32
BF16 = mybir.dt.bfloat16
I32 = mybir.dt.int32
U8 = mybir.dt.uint8
ALU = mybir.AluOpType
ACT = mybir.ActivationFunctionType
AX = mybir.AxisListType

P = 128


def bass_xattn_moe_twice(nc, x, ctx_in, bias, attn_mask, mask, pad_mask,
                         w0, b0, w_router, wi, wo, w1, b1, gate_w, gate_b, expert_w, expert_b, out):
    B, S, D = x.shape
    H, J = bias.shape[1], bias.shape[3]
    DK = D // H
    NE, _, F = wi.shape
    NG = gate_w.shape[0]
    CAP = 64
    NT = S // P
    FC = F // P
    HJ = H * J
    NC = -(-HJ // P)
    HJP = NC * P
    HB = 512 // J
    BANKS = [(0, HB), (HB, 2 * HB), (2 * HB, H)]
    H0 = [min(P * c // J, H - 3) for c in range(NC)]
    VW = 3 * (DK + 1)
    SCALE = float(DK) ** -0.5
    EPS = 1e-5
    MASKED = -1e9
    LAYERS = 2
    ROUTE0, ROUTE1 = 18, 24

    ctx = ExitStack()
    with ctx:
        def sb(name, shape, dt=F32):
            return ctx.enter_context(nc.sbuf_tensor(name, shape, dt))

        def bank(name, shape):
            return ctx.enter_context(nc.psum_tensor(name, shape, F32))

        def sem(name):
            return ctx.enter_context(nc.semaphore(name))

        X = sb("X", [P, B, NT, D])
        ident = sb("ident", [P, P])
        incl = sb("incl", [P, P], BF16)
        strict = sb("strict", [P, P], BF16)
        ones = sb("ones", [P, P], BF16)
        iota1 = sb("iota1", [P, CAP])
        rank = sb("rank", [P, NG])
        half = sb("half", [P, NT])
        headmask = sb("headmask", [P, H])
        rowmask = sb("rowmask", [P, NC, 3])
        W = sb("W", [P, 8, D])
        WT = sb("WT", [P, 8, D])
        bcol = sb("bcol", [P, 6])
        bo = sb("bo", [P, LAYERS, D])
        ctxn = sb("ctxn", [J, B, D])
        ctxT = sb("ctxT", [P, B, J])
        ctxR = sb("ctxR", [P, HJP])
        kT = sb("kT", [P, LAYERS, B, J])
        KB = sb("KB", [P, 2 * B, HJ])
        VB = sb("VB", [P, 2 * B, NC, VW])
        am = sb("am", [P, NT, J])
        padw = sb("padw", [P, B * J // 4], I32)
        padb = padw[:].bitcast(U8).rearrange("p (b j) -> p b j", b=B)
        padn = sb("padn", [P, B, J])
        amp = sb("amp", [P, NT, J])
        BI = [sb(f"BI{g}", [P, H, 2, J]) for g in range(2)]
        MI = [sb(f"MI{g}", [P, 2, J], I32) for g in range(2)]
        MN = [sb(f"MN{g}", [P, 2, J]) for g in range(2)]
        wi_s = sb("wi_s", [P, NE, F])
        wo_s = sb("wo_s", [P, NE, FC, D])
        wr_s = sb("wr_s", [P, NE])
        gw_s = sb("gw_s", [NG, D])
        gwT = sb("gwT", [P, NG])
        gb_s = sb("gb_s", [P, NG])
        ew_s = sb("ew_s", [P, NE, D])
        eb_s = sb("eb_s", [NT * NE, NT, D])

        a_st = sb("a_st", [P, NT, 6])
        a_mv = sb("a_mv", [P, NT, 2])
        a_ve = sb("a_ve", [P, NT])
        a_rs = sb("a_rs", [P, NT])
        a_xn = sb("a_xn", [P, NT, D])
        a_xT = sb("a_xT", [P, S])
        qT = sb("qT", [P, S])
        xr = sb("xr", [P, NT, D])
        SC = [sb(f"SC{n}", [P, HJP]) for n in range(2)]
        mx = sb("mx", [P, H])
        PT = sb("PT", [P, NC, P])
        rc = sb("rc", [P, H])
        o_n = sb("o_n", [P, D])
        oT = sb("oT", [P, P])

        f_st = sb("f_st", [P, NT, 6])
        f_mv = sb("f_mv", [P, NT, 2])
        f_ve = sb("f_ve", [P, NT])
        f_rs = sb("f_rs", [P, NT])
        f_xn = sb("f_xn", [P, NT, D])
        f_xT = sb("f_xT", [P, S])
        xh = sb("xh", [P, NT, D], BF16)
        xm = sb("xm", [P, NT, D], BF16)
        xl = sb("xl", [P, NT, D], BF16)
        xres = sb("xres", [P, NT, D])
        r_m = sb("r_m", [P, NT])
        r_l = sb("r_l", [P, NT, NG])
        r_e = sb("r_e", [P, NT, NG])
        r_s = sb("r_s", [P, NT])
        r_r = sb("r_r", [P, NT])
        r_p = sb("r_p", [P, NT, NG])
        r_p2 = sb("r_p2", [P, NT, NG])
        r_q = sb("r_q", [P, NT, NG])
        r_k = sb("r_k", [P, NT, NG])
        oh = sb("oh", [P, NT, 2, NE], BF16)
        oh1 = sb("oh1", [P, NT, 2, NG])
        r_c = sb("r_c", [P, NT, 2, NE])
        prio = sb("prio", [P, NT, NE])
        Dm = sb("Dm", [P, NT, NE, CAP], BF16)
        Cm = sb("Cm", [P, 2, NE, CAP])
        CT = sb("CT", [P, NT, NE // 2, P])
        ein = sb("ein", [P, NE, 2, CAP])
        hT = [sb(f"hT{n}", [P, FC, 2, CAP]) for n in range(2)]
        eo = sb("eo", [P, NE // 2, 2, D])
        cw = sb("cw", [P, NT, NE])
        cwT = sb("cwT", [NT * NE, P])
        acc = sb("acc", [P, NT, D])

        SP3 = bank("SP3", [P, 3, 512])
        TB = [bank(f"TB{n}", [P, 512]) for n in range(2)]
        MB = bank("MB", [P, 512])
        HBK = bank("HBK", [P, 512])
        EBK = bank("EBK", [P, 512])

        names = """ld_ctx ld_x ld_w ld_vec ld_moe ld_am ld_e1 st_out
        c_set c_ok c_idn k_ctxT k_ctxTs k_w k_ws k_kT k_kTs k_rep k_v k_vb k_kb k_pad k_gw k_gws k_eb0 k_eb
        a_stats a_aggr a_veps a_rstd a_xnok a_xTok a_xTs a_qok a_qTs a_xrok
        biasok0 biasok1 mneg masked0 masked1 ampok
        scores added rawmax rowmax shifted probs trE PTs pv recips normed oTok oTs proj resid
        f_stats f_aggr f_veps f_rstd f_xnok f_xTok f_xTs
        m_logits m_route m_exp m_cum m_split m_D m_C m_disp m_eins m_CT m_CTs m_h m_hs m_eo m_eos m_comb m_out
        n_logits n_route n_exp n_cwT n_cwTs n_bias n_eo n_used n_acc n_sum""".split()
        s = {n: sem(n) for n in names}

        def static_first(run):
            return isinstance(run, int) and run == 0

        def wait_alone(eng, *waits):
            held = [(q, v if isinstance(v, int) else eng.to_reg(v)) for q, v in waits]
            eng.wait_ge(s["c_idn"], 1)
            for q, v in held:
                eng.wait_ge(q, v)

        def sl(t, run):
            return t[:, bass.ds(run, 1)]

        x_v = x.rearrange("b (g p r) d -> b p g r d", g=2, r=2)
        out_v = out.rearrange("b (g p r) d -> b p g r d", g=2, r=2)
        am_v = attn_mask.rearrange("(g p r) j -> p g r j", g=2, r=2)
        bias_v = bias.rearrange("b h (g p r) j -> b g p h (r j)", g=2, r=2)
        mask_v = mask.rearrange("b (g p r) j -> b g p (r j)", g=2, r=2)

        block = ctx.enter_context(nc.Block())

        @block.sync
        def _(sp):
            sp.dma_start(ctxn[:], ctx_in.rearrange("b j d -> j b d")).then_inc(s["ld_ctx"], 16)
            for n in range(4):
                sp.dma_start(W[:, n, :], w0[n]).then_inc(s["ld_w"], 16)
            for n in range(4):
                sp.dma_start(W[:, 4 + n, :], w1[n]).then_inc(s["ld_w"], 16)
            for b in range(B):
                sp.dma_start(X[:, b].rearrange("p (g r) d -> p g r d", g=2), x_v[b]).then_inc(s["ld_x"], 16)

            def load_bias(a):
                for g, (ok, free) in enumerate((("biasok0", None), ("biasok1", None))):
                    if not static_first(a):
                        wait_alone(sp, (s["added"], (a - 1) * 2 * NT + 4 * (g + 1)),
                                   (s["mneg"], (a - 1) * 2 + g + 1))
                    src_b = bias_v[bass.ds(a, 1), g].rearrange("o p h rj -> (o p) h rj")
                    src_m = mask_v[bass.ds(a, 1), g].rearrange("o p rj -> (o p) rj")
                    sp.dma_start(BI[g][:].rearrange("p h r j -> p h (r j)"), src_b).then_inc(s[ok], 16)
                    sp.dma_start(MI[g][:].rearrange("p r j -> p (r j)"), src_m).then_inc(s[ok], 16)

            load_bias(0)
            sp.dma_start(wi_s[:], wi.rearrange("e d f -> d e f")).then_inc(s["ld_moe"], 16)
            sp.dma_start(wo_s[:], wo.rearrange("e (c f) d -> f e c d", c=FC)).then_inc(s["ld_moe"], 16)
            sp.dma_start(wr_s[:], w_router).then_inc(s["ld_moe"], 16)
            sp.dma_start(am[:].rearrange("p (g r) j -> p g r j", g=2), am_v).then_inc(s["ld_am"], 16)
            sp.dma_start(padw[:], pad_mask.partition_broadcast(P)).then_inc(s["ld_am"], 16)
            sp.dma_start(ew_s[:], expert_w.rearrange("e d h -> d e h")).then_inc(s["ld_e1"], 16)
            with sp.Fori(1, B) as a:
                load_bias(a)

            def store(f):
                b = f - B
                wait_alone(sp, (s["n_used"], 2 * NT * (b + 1)))
                sp.dma_start(out_v[bass.ds(b, 1)].rearrange("o p g r d -> (o p) g r d"),
                             acc[:].rearrange("p (g r) d -> p g r d", g=2)).then_inc(s["st_out"], 16)

            store(B)
            with sp.Fori(1, B) as f:
                store(f + B)
            sp.wait_ge(s["st_out"], 16 * B)

        @block.gpsimd
        def _(pool):
            g = nc.gpsimd
            g.memset(ident[:], 0.0).then_inc(s["c_set"], 1)
            pool.wait_ge(s["c_set"], 1)
            g.affine_select(out=ident[:], in_=ident[:], compare_op=ALU.not_equal, fill=1.0, base=0,
                            pattern=[[-1, P]], channel_multiplier=1).then_inc(s["c_idn"], 1)
            n_set = 1
            for t, v in ((headmask, 1.0), (rowmask, 1.0), (ones, 1.0), (incl, 1.0), (strict, 1.0),
                         (half, -0.5), (eb_s, 0.0), (ctxR, 0.0), (SC[0], 0.0), (SC[1], 0.0)):
                g.memset(t[:], v).then_inc(s["c_set"], 1)
                n_set += 1
            g.iota(iota1[:], pattern=[[1, CAP]], base=1, channel_multiplier=0,
                   allow_small_or_imprecise_dtypes=True).then_inc(s["c_ok"], 1)
            g.iota(rank[:], pattern=[[-1, NG]], base=NG, channel_multiplier=0,
                   allow_small_or_imprecise_dtypes=True).then_inc(s["c_ok"], 1)
            pool.wait_ge(s["c_set"], n_set)
            g.affine_select(out=headmask[:], in_=headmask[:], compare_op=ALU.is_ge, fill=0.0, base=0,
                            pattern=[[-DK, H]], channel_multiplier=1).then_inc(s["c_ok"], 1)
            pool.wait_ge(s["c_ok"], 3)
            g.affine_select(out=headmask[:], in_=headmask[:], compare_op=ALU.is_ge, fill=0.0, base=DK - 1,
                            pattern=[[DK, H]], channel_multiplier=-1).then_inc(s["c_ok"], 1)
            g.affine_select(out=incl[:], in_=incl[:], compare_op=ALU.is_ge, fill=0.0, base=0,
                            pattern=[[1, P]], channel_multiplier=-1).then_inc(s["c_ok"], 1)
            g.affine_select(out=strict[:], in_=strict[:], compare_op=ALU.is_ge, fill=0.0, base=-1,
                            pattern=[[1, P]], channel_multiplier=-1).then_inc(s["c_ok"], 1)
            for c in range(NC):
                g.affine_select(out=rowmask[:, c, :], in_=rowmask[:, c, :], compare_op=ALU.is_ge, fill=0.0,
                                base=P * c - J * H0[c], pattern=[[-J, 3]],
                                channel_multiplier=1).then_inc(s["c_ok"], 1)
            pool.wait_ge(s["c_ok"], 6 + NC)
            for c in range(NC):
                g.affine_select(out=rowmask[:, c, :], in_=rowmask[:, c, :], compare_op=ALU.is_ge, fill=0.0,
                                base=J * H0[c] + J - 1 - P * c, pattern=[[J, 3]],
                                channel_multiplier=-1).then_inc(s["c_ok"], 1)

            for n, v in enumerate((b0[0], b0[1], b0[2], b1[0], b1[1], b1[2])):
                g.dma_start(bcol[:, n:n + 1], v.rearrange("(p o) -> p o", o=1)).then_inc(s["ld_vec"], 16)
            g.dma_start(bo[:, 0, :], b0[3].partition_broadcast(P)).then_inc(s["ld_vec"], 16)
            g.dma_start(bo[:, 1, :], b1[3].partition_broadcast(P)).then_inc(s["ld_vec"], 16)
            g.dma_start(gb_s[:], gate_b.partition_broadcast(P)).then_inc(s["ld_vec"], 16)
            g.dma_start(gw_s[:], gate_w).then_inc(s["ld_vec"], 16)
            for i in range(NT):
                g.dma_start(eb_s[NE * i:NE * (i + 1), i, :], expert_b).then_inc(s["ld_vec"], 16)

            def rstd(aggr, mv, ve, rs, okv, okr, run):
                wait_alone(pool, (s[aggr], NT * (run + 1)))
                g.tensor_scalar(ve[:], mv[:, :, 1], EPS, None, ALU.add).then_inc(s[okv], 1)
                pool.wait_ge(s[okv], run + 1)
                g.tensor_tensor(rs[:], ve[:], half[:], ALU.pow).then_inc(s[okr], 1)

            def a_rstd(a):
                rstd("a_aggr", a_mv, a_ve, a_rs, "a_veps", "a_rstd", a)

            def f_rstd(f):
                rstd("f_aggr", f_mv, f_ve, f_rs, "f_veps", "f_rstd", f)

            def residual_bias(a, layer):
                if layer == 0:
                    pool.wait_ge(s["ld_x"], 16 * B)
                    pool.wait_ge(s["ld_vec"], 16 * 14)
                else:
                    pool.wait_ge(s["m_out"], a - B + 1)
                if not static_first(a):
                    pool.wait_ge(s["resid"], NT * a)
                xin = sl(X, a - B * layer).rearrange("p o i d -> p (o i) d")
                g.tensor_tensor(xr[:], xin, bo[:, layer:layer + 1, :].broadcast_to([P, NT, D]),
                                ALU.add).then_inc(s["a_xrok"], 1)

            def mask_bias(a, gi):
                wait_alone(pool, (s[f"biasok{gi}"], 32 * (a + 1)), *([] if static_first(a) else [(s[f"masked{gi}"], a)]))
                g.tensor_scalar(MN[gi][:], MI[gi][:], 0, 2 * MASKED, ALU.is_equal, ALU.mult).then_inc(s["mneg"], 1)
                pool.wait_ge(s["mneg"], 2 * a + gi + 1)
                g.tensor_tensor(BI[gi][:].rearrange("p h r j -> p h (r j)"),
                                BI[gi][:].rearrange("p h r j -> p h (r j)"),
                                MN[gi][:].rearrange("p r j -> p (r j)").unsqueeze(1).broadcast_to([P, H, 2 * J]),
                                ALU.add).then_inc(s[f"masked{gi}"], 1)

            def mask_attn(a):
                b = a - B
                if not static_first(b):
                    pool.wait_ge(s["added"], 2 * NT * a)
                g.tensor_tensor(amp[:], am[:], sl(padn, b).broadcast_to([P, NT, J]), ALU.add)\
                    .then_inc(s["ampok"], 1)

            def split_x(f):
                wait_alone(pool, (s["f_xnok"], NT * (f + 1)), *([] if static_first(f) else [(s["m_disp"], 2 * f)]))
                base = 4 * f
                g.tensor_copy(xh[:], f_xn[:]).then_inc(s["m_split"], 1)
                pool.wait_ge(s["m_split"], base + 1)
                g.tensor_tensor(xres[:], f_xn[:], xh[:], ALU.subtract).then_inc(s["m_split"], 1)
                wait_alone(pool, (s["m_split"], base + 2))
                g.tensor_copy(xm[:], xres[:]).then_inc(s["m_split"], 1)
                pool.wait_ge(s["m_split"], base + 3)
                g.tensor_tensor(xl[:], xres[:], xm[:], ALU.subtract).then_inc(s["m_split"], 1)

            def combine_weights(f):
                for i in range(NT):
                    pool.wait_ge(s["m_D"], 2 * f + i // 2 + 1)
                    if i >= 2 or not static_first(f):
                        pool.wait_ge(s["m_CT"], NT * f + i - 1)
                    g.tensor_tensor(Cm[:, i % 2], Dm[:, i],
                                    r_p[:, i, 0:NE].unsqueeze(2).broadcast_to([P, NE, CAP]),
                                    ALU.mult).then_inc(s["m_C"], 1)

            def step0(a, f):
                if a is not None:
                    a_rstd(a)
                if f is not None:
                    f_rstd(f)
                if a is not None:
                    residual_bias(a, 0)
                    mask_bias(a, 0)
                    mask_bias(a, 1)
                if f is not None:
                    split_x(f)
                    combine_weights(f)

            def step1(a, f):
                if a is not None:
                    a_rstd(a)
                if f is not None:
                    f_rstd(f)
                if a is not None:
                    residual_bias(a, 1)
                    mask_attn(a)

            step0(0, None)
            step0(1, 0)
            with pool.Fori(1, B - 1) as n:
                step0(n + 1, n)
            pool.wait_ge(s["ld_am"], 32)
            g.tensor_scalar(padn[:], padb, -3e38, 2.0, ALU.mult, ALU.mult).then_inc(s["k_pad"], 1)
            pool.wait_ge(s["k_pad"], 1)
            a_rstd(B)
            f_rstd(B - 1)
            residual_bias(B, 1)
            mask_attn(B)
            split_x(B - 1)
            combine_weights(B - 1)
            step1(B + 1, B)
            with pool.Fori(1, B - 1) as n:
                step1(n + B + 1, n + B)
            f_rstd(2 * B - 1)

        @block.scalar
        def _(act):
            sc = nc.scalar
            act.wait_ge(s["k_ctxT"], 1)
            sc.copy(ctxT[:].rearrange("p b j -> p (b j)"), MB[:, 0:B * J]).then_inc(s["k_ctxTs"], 1)
            for n in range(2):
                act.wait_ge(s["k_w"], n + 1)
                sc.copy(WT[:, 4 * n:4 * n + 4, :].rearrange("p n d -> p (n d)"), [HBK, EBK][n][:])\
                    .then_inc(s["k_ws"], 1)
            act.wait_ge(s["ld_vec"], 16 * 14)
            for n in range(2):
                act.wait_ge(s["k_kT"], n + 1)
                sc.activation(kT[:, n].rearrange("p b j -> p (b j)"), SP3[:, n, 0:B * J], ACT.Identity,
                              bias=bcol[:, 3 * n + 1:3 * n + 2]).then_inc(s["k_kTs"], 1)
            act.wait_ge(s["k_gw"], 1)
            sc.copy(gwT[:], SP3[:, 2, 0:NG]).then_inc(s["k_gws"], 1)

            def a_xTcopy(a):
                act.wait_ge(s["a_xTok"], a + 1)
                sc.copy(a_xT[:], MB[:]).then_inc(s["a_xTs"], 1)

            def f_xTcopy(f):
                act.wait_ge(s["f_xTok"], f + 1)
                sc.copy(f_xT[:], HBK[:]).then_inc(s["f_xTs"], 1)

            def softmax_exp(a, i):
                act.wait_ge(s["shifted"], NT * a + i + 1)
                sc.activation(SC[i % 2][:, 0:HJ], SC[i % 2][:, 0:HJ], ACT.Exp).then_inc(s["probs"], 1)

            def copy_PT(a, i):
                t = NT * a + i
                for n, (c0, c1) in enumerate(((0, 4), (4, 8), (8, NC))):
                    act.wait_ge(s["trE"], 3 * t + n + 1)
                    if n == 0 and not static_first(a if i == 0 else 1):
                        act.wait_ge(s["pv"], t)
                    sc.copy(PT[:, c0:c1, :].rearrange("p c t -> p (c t)"),
                            TB[n % 2][:, 0:(c1 - c0) * P]).then_inc(s["PTs"], 1)

            def copy_oT(a, i, layer):
                act.wait_ge(s["oTok"], NT * a + i + 1)
                sc.activation(oT[:], MB[:, 0:P], ACT.Identity,
                              bias=bcol[:, 3 * layer + 2:3 * layer + 3]).then_inc(s["oTs"], 1)

            def route_exp(route, per, k, ok, ne, run):
                act.wait_ge(s[route], per * run + k)
                sc.activation(r_e[:, :, 0:ne], r_l[:, :, 0:ne], ACT.Exp).then_inc(s[ok], 1)

            def copy_ein(f):
                for g in range(2):
                    act.wait_ge(s["m_disp"], 2 * f + g + 1)
                    sc.copy(ein[:, :, g, :], [HBK, EBK][g][:].rearrange("p (e c) -> p e c", e=NE))\
                        .then_inc(s["m_eins"], 1)

            def copy_CT(f):
                for i in range(NT):
                    act.wait_ge(s["m_CT"], NT * f + i + 1)
                    sc.copy(CT[:, i].rearrange("p k t -> p (k t)"), [HBK, EBK][i % 2][:]).then_inc(s["m_CTs"], 1)

            def gelu(f, e):
                act.wait_ge(s["m_h"], NE * f + e + 1)
                sc.activation(hT[e % 2][:].rearrange("p c g s -> p (c g s)"), HBK[:], ACT.Gelu_apprx_tanh)\
                    .then_inc(s["m_hs"], 1)

            def copy_eo(f, k):
                act.wait_ge(s["m_eo"], NE // 2 * f + k + 1)
                sc.copy(eo[:, k].rearrange("p g d -> p (g d)"), EBK[:, 0:2 * D]).then_inc(s["m_eos"], 1)

            def burst(f, n):
                k = 2 * n
                gelu(f, 2 * k)
                gelu(f, 2 * k + 1)
                gelu(f, 2 * k + 2)
                copy_eo(f, k)
                gelu(f, 2 * k + 3)
                copy_eo(f, k + 1)

            def step0(a, f, layer=0):
                A, M = a is not None, f is not None
                if A:
                    a_xTcopy(a)
                if M:
                    f_xTcopy(f)
                    route_exp("m_route", ROUTE0, 2, "m_exp", NE, f)
                if A:
                    softmax_exp(a, 0)
                    copy_PT(a, 0)
                if M:
                    copy_ein(f)
                if A:
                    softmax_exp(a, 1)
                    copy_oT(a, 0, layer)
                    copy_PT(a, 1)
                if M:
                    copy_CT(f)
                    burst(f, 0)
                if A:
                    softmax_exp(a, 2)
                    copy_oT(a, 1, layer)
                    copy_PT(a, 2)
                    softmax_exp(a, 3)
                    copy_oT(a, 2, layer)
                    copy_PT(a, 3)
                if M:
                    burst(f, 1)
                if A:
                    copy_oT(a, 3, layer)

            def copy_cwT(f):
                act.wait_ge(s["n_cwT"], f - B + 1)
                sc.copy(cwT[:], EBK[0:NT * NE, 0:P]).then_inc(s["n_cwTs"], 1)

            def step1(a, f):
                A, M = a is not None, f is not None
                if A:
                    a_xTcopy(a)
                if M:
                    f_xTcopy(f)
                    route_exp("n_route", ROUTE1, 3, "n_exp", NG, f - B)
                if A:
                    softmax_exp(a, 0)
                    copy_PT(a, 0)
                if M:
                    copy_cwT(f)
                if A:
                    for i in range(1, NT):
                        softmax_exp(a, i)
                        copy_oT(a, i - 1, 1)
                        copy_PT(a, i)
                    copy_oT(a, NT - 1, 1)

            step0(0, None)
            step0(1, 0)
            with act.Fori(1, B - 1) as n:
                step0(n + 1, n)
            step0(B, B - 1, layer=1)
            step1(B + 1, B)
            with act.Fori(1, B - 1) as n:
                step1(n + B + 1, n + B)
            step1(None, 2 * B - 1)

        @block.tensor
        def _(pe):
            te = nc.tensor
            pe.wait_ge(s["c_idn"], 1)
            pe.wait_ge(s["ld_ctx"], 16)
            for b in range(B):
                last = te.transpose(MB[:, b * J:(b + 1) * J], ctxn[:, b, :], ident[0:J, 0:J])
            last.then_inc(s["k_ctxT"], 1)
            pe.wait_ge(s["ld_w"], 16 * 8)
            for n in range(8):
                last = te.transpose([HBK, EBK][n // 4][:, (n % 4) * D:(n % 4 + 1) * D], W[:, n, :], ident[:])
                if n % 4 == 3:
                    last.then_inc(s["k_w"], 1)
            pe.wait_ge(s["k_ctxTs"], 1)
            pe.wait_ge(s["k_ws"], 2)
            for n in range(2):
                te.matmul(SP3[:, n, 0:B * J], WT[:, 4 * n + 1, :], ctxT[:].rearrange("p b j -> p (b j)"),
                          start=True, stop=True).then_inc(s["k_kT"], 1)
            pe.wait_ge(s["ld_vec"], 16 * 14)
            te.transpose(SP3[:, 2, 0:NG], gw_s[:], ident[0:NG, 0:NG]).then_inc(s["k_gw"], 1)

            def values(b):
                pe.wait_ge(s["k_rep"], b + 1)
                if not static_first(b):
                    pe.wait_ge(s["k_vb"], 4 * b)
                for n in range(LAYERS):
                    for c in range(NC):
                        last = te.matmul(TB[n][:, 3 * DK * c:3 * DK * (c + 1)], ctxR[:, c * P:(c + 1) * P],
                                         WT[:, 4 * n + 2, DK * H0[c]:DK * (H0[c] + 3)], start=True, stop=True)
                    last.then_inc(s["k_v"], 1)

            values(0)
            with pe.Fori(1, B) as b:
                values(b)
            pe.wait_ge(s["k_vb"], 4 * B)

            def a_xTr(a):
                for i in range(NT):
                    pe.wait_ge(s["a_xnok"], NT * a + i + 1)
                    if i == 0 and not static_first(a):
                        pe.wait_ge(s["resid"], NT * a)
                    last = te.transpose(MB[:, i * P:(i + 1) * P], a_xn[:, i, :], ident[:])
                last.then_inc(s["a_xTok"], 1)

            def query(a, layer):
                pe.wait_ge(s["a_xTs"], a + 1)
                te.matmul(MB[:], WT[:, 4 * layer, :], a_xT[:], start=True, stop=True).then_inc(s["a_qok"], 1)

            def attn_scores(a, i):
                t = NT * a + i
                if i == 0:
                    pe.wait_ge(s["a_qTs"], a + 1)
                kb = sl(KB, a).rearrange("p o n -> p (o n)")
                for n, (h0, h1) in enumerate(BANKS):
                    if n != 1 and not static_first(a if i == 0 else 1):
                        pe.wait_ge(s["added"], 2 * (t - 1) + (1 if n == 0 else 2))
                    last = te.matmul(SP3[:, n, 0:(h1 - h0) * J], qT[:, i * P:(i + 1) * P],
                                     kb[:, h0 * J:h1 * J], start=True, stop=True)
                    if n > 0:
                        last.then_inc(s["scores"], 1)

            def turn_probs(a, i, n, c0, c1):
                t = NT * a + i
                if n == 0:
                    pe.wait_ge(s["probs"], t + 1)
                if n == 0 and not static_first(a if i == 0 else 1):
                    pe.wait_ge(s["PTs"], 3 * t)
                if n == 2:
                    pe.wait_ge(s["PTs"], 3 * t + 1)
                for c in range(c0, c1):
                    last = te.transpose(TB[n % 2][:, (c - c0) * P:(c - c0 + 1) * P],
                                        SC[i % 2][:, c * P:(c + 1) * P], ident[:])
                last.then_inc(s["trE"], 1)

            def weigh_values(a, i):
                t = NT * a + i
                vb = sl(VB, a).rearrange("p o c v -> p (o c) v")
                pe.wait_ge(s["PTs"], 3 * t + 1)
                if i == 0:
                    pe.wait_ge(s["a_qTs"], a + 1)
                else:
                    pe.wait_ge(s["resid"], t)
                for c in range(NC):
                    if c == 4:
                        pe.wait_ge(s["PTs"], 3 * t + 2)
                    if c == 8:
                        pe.wait_ge(s["PTs"], 3 * t + 3)
                    last = te.matmul(MB[:, (DK + 1) * H0[c]:(DK + 1) * H0[c] + VW], PT[:, c, :], vb[:, c, :],
                                     start=(c == 0), stop=(c == NC - 1), skip_group_check=True)
                last.then_inc(s["pv"], 1)

            def turn_o(a, i):
                pe.wait_ge(s["normed"], NT * a + i + 1)
                te.transpose(MB[:, 0:P], o_n[:], ident[:]).then_inc(s["oTok"], 1)

            def project(a, i, layer):
                pe.wait_ge(s["oTs"], NT * a + i + 1)
                te.matmul(MB[:, 0:D], oT[:], WT[:, 4 * layer + 3, :], start=True, stop=True)\
                    .then_inc(s["proj"], 1)

            def attn_tile(a, i, layer):
                if i + 1 < NT:
                    attn_scores(a, i + 1)
                if i > 0:
                    turn_o(a, i - 1)
                turn_probs(a, i, 0, 0, 4)
                turn_probs(a, i, 1, 4, 8)
                if i > 0:
                    project(a, i - 1, layer)
                turn_probs(a, i, 2, 8, NC)
                weigh_values(a, i)

            def f_xTr(f, layer):
                for i in range(NT):
                    pe.wait_ge(s["f_xnok"], NT * f + i + 1)
                    if i == 0 and not static_first(f):
                        if layer == 0 or static_first(f - B):
                            pe.wait_ge(s["m_out"], f)
                        else:
                            pe.wait_ge(s["n_used"], 2 * NT * (f - B))
                    last = te.transpose(HBK[:, i * P:(i + 1) * P], f_xn[:, i, :], ident[:])
                last.then_inc(s["f_xTok"], 1)

            def logits0(f):
                pe.wait_ge(s["f_xTs"], f + 1)
                if static_first(f):
                    pe.wait_ge(s["ld_moe"], 48)
                for i in range(NT):
                    last = te.matmul(EBK[:, i * NE:(i + 1) * NE], f_xT[:, i * P:(i + 1) * P], wr_s[:],
                                     start=True, stop=True)
                last.then_inc(s["m_logits"], 1)

            def positions(f):
                pe.wait_ge(s["m_route"], ROUTE0 * f + 16)
                for g in range(2):
                    t0, t1 = 2 * g, 2 * g + 1
                    for i, first in ((t0, incl), (t1, incl)):
                        o = HBK[:, i * 2 * NE:(i + 1) * 2 * NE]
                        second = strict if i == t0 else incl
                        te.matmul(o, first[:], oh[:, t0].rearrange("p k e -> p (k e)"),
                                  start=True, stop=False, skip_group_check=True)
                        te.matmul(o, second[:], oh[:, t1].rearrange("p k e -> p (k e)"),
                                  start=False, stop=False, skip_group_check=True)
                        te.matmul(o[:, NE:], ones[:], oh[:, t0, 0, :], start=False, stop=False,
                                  skip_group_check=True)
                        last = te.matmul(o[:, NE:], ones[:], oh[:, t1, 0, :], start=False, stop=True,
                                         skip_group_check=True)
                last.then_inc(s["m_cum"], 1)

            def dispatch(f):
                pe.wait_ge(s["m_split"], 4 * f + 4)
                for g in range(2):
                    pe.wait_ge(s["m_D"], 2 * f + g + 1)
                    n = 0
                    for i in (2 * g, 2 * g + 1):
                        for part in (xh, xm, xl):
                            last = te.matmul([HBK, EBK][g][:], part[:, i, :],
                                             Dm[:, i].rearrange("p e c -> p (e c)"),
                                             start=(n == 0), stop=(n == 5))
                            n += 1
                    last.then_inc(s["m_disp"], 1)

            def turn_C(f):
                for i in range(NT):
                    pe.wait_ge(s["m_C"], NT * f + i + 1)
                    if i < 2:
                        pe.wait_ge(s["m_eins"], 2 * f + i + 1)
                    else:
                        pe.wait_ge(s["m_CTs"], NT * f + i - 1)
                    for k in range(NE // 2):
                        last = te.transpose([HBK, EBK][i % 2][:, k * P:(k + 1) * P],
                                            Cm[:, i % 2, 2 * k:2 * k + 2, :].rearrange("p e c -> p (e c)"), ident[:])
                    last.then_inc(s["m_CT"], 1)

            def up(f, e):
                if e == 0:
                    pe.wait_ge(s["m_CTs"], NT * f + NT)
                else:
                    pe.wait_ge(s["m_hs"], NE * f + e)
                for c in range(FC):
                    last = te.matmul(HBK[:, c * P:(c + 1) * P], wi_s[:, e, c * P:(c + 1) * P],
                                     ein[:, e].rearrange("p g c -> p (g c)"), start=True, stop=True)
                last.then_inc(s["m_h"], 1)

            def down(f, k, g):
                if g == 0:
                    pe.wait_ge(s["m_hs"], NE * f + 2 * k + 2)
                    if k > 0:
                        pe.wait_ge(s["m_eos"], NE // 2 * f + k)
                for c in range(FC):
                    for q in range(2):
                        last = te.matmul(EBK[q * CAP:(q + 1) * CAP, g * D:(g + 1) * D], hT[q][:, c, g, :],
                                         wo_s[:, 2 * k + q, c, :], start=(c == 0), stop=(c == FC - 1))
                if g == 1:
                    last.then_inc(s["m_eo"], 1)

            def burst(f, n):
                k = 2 * n
                up(f, 2 * k)
                up(f, 2 * k + 1)
                down(f, k, 0)
                down(f, k, 1)
                up(f, 2 * k + 2)
                up(f, 2 * k + 3)
                down(f, k + 1, 0)
                down(f, k + 1, 1)

            def combine(f):
                pe.wait_ge(s["m_eos"], NE // 2 * (f + 1))
                for i in range(NT):
                    for k in range(NE // 2):
                        last = te.matmul(HBK[:, i * D:(i + 1) * D], CT[:, i, k, :], eo[:, k, i // 2, :],
                                         start=(k == 0), stop=(k == NE // 2 - 1))
                last.then_inc(s["m_comb"], 1)

            def step0(a, f, layer=0):
                A, M = a is not None, f is not None
                if A:
                    a_xTr(a)
                if M:
                    f_xTr(f, 0)
                if A:
                    query(a, layer)
                if M:
                    logits0(f)
                if A:
                    attn_scores(a, 0)
                if M:
                    positions(f)
                if A:
                    attn_tile(a, 0, layer)
                if M:
                    dispatch(f)
                if A:
                    attn_tile(a, 1, layer)
                if M:
                    turn_C(f)
                    burst(f, 0)
                if A:
                    attn_tile(a, 2, layer)
                    attn_tile(a, 3, layer)
                if M:
                    burst(f, 1)
                    combine(f)
                if A:
                    turn_o(a, NT - 1)
                    project(a, NT - 1, layer)

            def logits1(f):
                pe.wait_ge(s["f_xTs"], f + 1)
                if static_first(f - B):
                    pe.wait_ge(s["k_gws"], 1)
                    pe.wait_ge(s["ld_e1"], 16)
                for i in range(NT):
                    last = te.matmul(EBK[:, i * NG:(i + 1) * NG], f_xT[:, i * P:(i + 1) * P], gwT[:],
                                     start=True, stop=True)
                last.then_inc(s["n_logits"], 1)

            def expert_bias(f):
                m = f - B
                pe.wait_ge(s["n_route"], ROUTE1 * (m + 1))
                te.transpose(EBK[0:NT * NE, 0:P], cw[:].rearrange("p i e -> p (i e)"), ident[:])\
                    .then_inc(s["n_cwT"], 1)
                pe.wait_ge(s["n_cwTs"], m + 1)
                te.matmul(EBK[:], cwT[:], eb_s[:].rearrange("k i d -> k (i d)"), start=True, stop=True)\
                    .then_inc(s["n_bias"], 1)

            def experts(f, i):
                m = f - B
                for n in range(2):
                    if i == 0:
                        pe.wait_ge(s["n_acc"], m + 1)
                    else:
                        pe.wait_ge(s["n_used"], 2 * NT * m + 2 * (i - 1) + n + 1)
                    te.matmul([HBK, EBK][n][:], f_xT[:, i * P:(i + 1) * P],
                              ew_s[:, 4 * n:4 * n + 4, :].rearrange("p e d -> p (e d)"),
                              start=True, stop=True).then_inc(s["n_eo"], 1)

            def step1(a, f):
                A, M = a is not None, f is not None
                if A:
                    a_xTr(a)
                if M:
                    f_xTr(f, 1)
                if A:
                    query(a, 1)
                if M:
                    logits1(f)
                if A:
                    attn_scores(a, 0)
                if M and not A:
                    expert_bias(f)
                for i in range(NT):
                    if A:
                        attn_tile(a, i, 1)
                    if M:
                        if i == 0 and A:
                            expert_bias(f)
                        experts(f, i)
                if A:
                    turn_o(a, NT - 1)
                    project(a, NT - 1, 1)

            step0(0, None)
            step0(1, 0)
            with pe.Fori(1, B - 1) as n:
                step0(n + 1, n)
            step0(B, B - 1, layer=1)
            step1(B + 1, B)
            with pe.Fori(1, B - 1) as n:
                step1(n + B + 1, n + B)
            step1(None, 2 * B - 1)

        @block.vector
        def _(dve):
            v = nc.vector
            dve.wait_ge(s["c_ok"], 6 + 2 * NC)

            def block_kv(b):
                if static_first(b):
                    dve.wait_ge(s["k_ctxTs"], 1)
                else:
                    dve.wait_ge(s["k_v"], 2 * b)
                v.tensor_copy(ctxR[:, 0:HJ].rearrange("p (h j) -> p h j", h=H),
                              sl(ctxT, b).broadcast_to([P, H, J])).then_inc(s["k_rep"], 1)
                if static_first(b):
                    dve.wait_ge(s["k_kTs"], 2)
                for n in range(LAYERS):
                    v.tensor_tensor(sl(KB, b + n * B).rearrange("p o (h j) -> p (o h) j", h=H),
                                    kT[:, n, bass.ds(b, 1), :].broadcast_to([P, H, J]),
                                    headmask[:].unsqueeze(2).broadcast_to([P, H, J]), ALU.mult)\
                        .then_inc(s["k_kb"], 1)
                for n in range(LAYERS):
                    dve.wait_ge(s["k_v"], 2 * b + n + 1)
                    vb = sl(VB, b + n * B).rearrange("p o c (h d) -> p (o c h) d", h=3)
                    rm = rowmask[:].rearrange("p c h -> p (c h)").unsqueeze(2)
                    v.tensor_tensor(vb[:, :, 0:DK], TB[n][:, 0:NC * 3 * DK].rearrange("p (n d) -> p n d", d=DK),
                                    rm.broadcast_to([P, 3 * NC, DK]), ALU.mult).then_inc(s["k_vb"], 1)
                    v.tensor_copy(vb[:, :, DK:DK + 1], rm).then_inc(s["k_vb"], 1)

            block_kv(0)
            with dve.Fori(1, B) as b:
                block_kv(b)
            dve.wait_ge(s["k_kb"], 2 * B)
            dve.wait_ge(s["k_vb"], 4 * B)

            def layer_norm(pre, st, mv, rs, xn, run, b, freed, split=None):
                xin = sl(X, b).rearrange("p o i d -> p (o i) d")
                for i in range(NT):
                    v.bn_stats(st[:, i, :], xin[:, i, :]).then_inc(s[pre + "_stats"], 1)
                for i in range(NT):
                    wait_alone(dve, (s[pre + "_stats"], NT * run + i + 1))
                    v.bn_aggr(mv[:, i, :], st[:, i, :]).then_inc(s[pre + "_aggr"], 1)
                if not static_first(run):
                    dve.wait_ge(s[freed], run)
                    if split is not None:
                        dve.wait_ge(s["m_split"], split)
                dve.wait_ge(s[pre + "_rstd"], run + 1)
                for i in range(NT):
                    v.tensor_scalar(xn[:, i, :], xin[:, i, :], mv[:, i, 0:1], rs[:, i:i + 1],
                                    ALU.subtract, ALU.mult).then_inc(s[pre + "_xnok"], 1)

            def a_norm(a, layer):
                if layer == 0:
                    if static_first(a):
                        dve.wait_ge(s["ld_x"], 16 * B)
                else:
                    dve.wait_ge(s["m_out"], a - B + 1)
                layer_norm("a", a_st, a_mv, a_rs, a_xn, a, a - B * layer, "a_xTok")

            def f_norm(f, layer):
                dve.wait_ge(s["resid"], NT * (f + 1))
                layer_norm("f", f_st, f_mv, f_rs, f_xn, f, f - B * layer, "f_xTok",
                           4 * f if layer == 0 else 4 * B)

            def scale_q(a, layer):
                dve.wait_ge(s["a_qok"], a + 1)
                v.tensor_scalar(qT[:], MB[:], bcol[:, 3 * layer:3 * layer + 1], SCALE, ALU.add, ALU.mult)\
                    .then_inc(s["a_qTs"], 1)

            def softmax_shift(a, i, layer):
                t = NT * a + i
                g, r = i // 2, i % 2
                S_ = SC[i % 2]
                if layer == 0 and r == 0:
                    dve.wait_ge(s[f"masked{g}"], a + 1)
                if layer == 1 and i == 0:
                    dve.wait_ge(s["ampok"], a - B + 1)
                if not static_first(a) or i >= 2:
                    dve.wait_ge(s["trE"], 3 * (t - 1))
                for n, (h0, h1, k) in enumerate(((0, 2 * HB, 2), (2 * HB, H, 1))):
                    dve.wait_ge(s["scores"], 2 * t + n + 1)
                    hh = (h1 - h0) // k
                    shape = [P, k, hh, J]
                    o = S_[:, h0 * J:h1 * J].rearrange("p (k h j) -> p k h j", k=k, h=hh)
                    i0 = SP3[:, 2 * n:2 * n + k, 0:hh * J].rearrange("p k (h j) -> p k h j", h=hh)
                    if layer == 0:
                        i1 = BI[g][:, h0:h1, r, :].rearrange("p (k h) j -> p k h j", k=k)
                    else:
                        i1 = amp[:, i:i + 1, :].unsqueeze(1).broadcast_to(shape)
                    v.tensor_tensor(o, i0, i1, ALU.add).then_inc(s["added"], 1)
                dve.wait_ge(s["added"], 2 * t + 2)
                S3 = S_[:, 0:HJ].rearrange("p (h j) -> p h j", h=H)
                mb = mx[:].unsqueeze(2).broadcast_to([P, H, J])
                if layer == 0:
                    v.tensor_reduce(mx[:], S3, AX.X, ALU.max).then_inc(s["rawmax"], 1)
                    dve.wait_ge(s["rawmax"], t + 1)
                    v.tensor_scalar(mx[:], mx[:], MASKED, None, ALU.max).then_inc(s["rowmax"], 1)
                    dve.wait_ge(s["rowmax"], t + 1)
                    v.scalar_tensor_tensor(S3, S3, MASKED, mb, ALU.max, ALU.subtract).then_inc(s["shifted"], 1)
                else:
                    v.tensor_reduce(mx[:], S3, AX.X, ALU.max).then_inc(s["rowmax"], 1)
                    dve.wait_ge(s["rowmax"], t + 1)
                    v.tensor_tensor(S3, S3, mb, ALU.subtract).then_inc(s["shifted"], 1)

            def normalise(a, i):
                t = NT * a + i
                dve.wait_ge(s["pv"], t + 1)
                pvv = MB[:, 0:H * (DK + 1)].rearrange("p (h d) -> p h d", h=H)
                v.reciprocal(rc[:].unsqueeze(2), pvv[:, :, DK:DK + 1]).then_inc(s["recips"], 1)
                dve.wait_ge(s["recips"], t + 1)
                v.tensor_tensor(o_n[:].rearrange("p (h d) -> p h d", h=H), pvv[:, :, 0:DK],
                                rc[:].unsqueeze(2).broadcast_to([P, H, DK]), ALU.mult).then_inc(s["normed"], 1)

            def add_residual(a, i, layer):
                dve.wait_ge(s["proj"], NT * a + i + 1)
                if i == 0:
                    dve.wait_ge(s["a_xrok"], a + 1)
                xo = sl(X, a - B * layer).rearrange("p o i d -> p (o i) d")
                v.tensor_tensor(xo[:, i, :], MB[:, 0:D], xr[:, i, :], ALU.add).then_inc(s["resid"], 1)

            def top2(step, ne, o1, o2, k, lg, exp_ok, run):
                nb = [P, NT, ne]
                l_, e_, p_, p2, q_, k_ = (z[:, :, 0:ne] for z in (r_l, r_e, r_p, r_p2, r_q, r_k))
                rk = rank[:, 0:ne].unsqueeze(1).broadcast_to(nb)
                bc = lambda z: z[:].unsqueeze(2).broadcast_to(nb)
                step(v.tensor_reduce(r_m[:], lg, AX.X, ALU.max))
                step(v.tensor_tensor(l_, lg, bc(r_m), ALU.subtract))
                dve.wait_ge(s[exp_ok], run + 1)
                step(v.tensor_reduce(r_s[:], e_, AX.X, ALU.add))
                step(v.reciprocal(r_r[:], r_s[:]))
                step(v.tensor_tensor(p_, e_, bc(r_r), ALU.mult))
                for n, (src, o) in enumerate(((p_, o1), (p2, o2))):
                    step(v.tensor_reduce(r_m[:], src, AX.X, ALU.max))
                    step(v.tensor_tensor(q_, src, bc(r_m), ALU.is_equal))
                    step(v.tensor_tensor(k_, q_, rk, ALU.mult))
                    step(v.tensor_reduce(r_s[:], k_, AX.X, ALU.max))
                    step(v.tensor_tensor(o, k_, bc(r_s), ALU.is_equal))
                    if n == 0:
                        step(v.scalar_tensor_tensor(p2, o, -2.0, p_, ALU.mult, ALU.add))

            class Steps:

                def __init__(self, name, base):
                    self.name, self.base, self.n = name, base, 0

                def __call__(self, ins):
                    self.n += 1
                    ins.then_inc(s[self.name], 1)
                    dve.wait_ge(s[self.name], self.base + self.n)

            def route0(f, st):
                dve.wait_ge(s["m_logits"], f + 1)
                top2(st, NE, oh[:, :, 0, :], oh[:, :, 1, :], 0,
                     EBK[:, 0:NT * NE].rearrange("p (i e) -> p i e", i=NT), "m_exp", f)

            def slots(f, st):
                dve.wait_ge(s["m_cum"], f + 1)
                st(v.tensor_tensor(r_c[:].rearrange("p i k e -> p (i k e)"), HBK[:, 0:NT * 2 * NE],
                                   oh[:].rearrange("p i k e -> p (i k e)"), ALU.mult))
                st(v.tensor_tensor(prio[:], r_c[:, :, 0, :], r_c[:, :, 1, :], ALU.add))
                for g in range(2):
                    shape = [P, 2 * NE, CAP]
                    v.tensor_tensor(Dm[:, 2 * g:2 * g + 2].rearrange("p i e c -> p (i e) c"),
                                    iota1[:].unsqueeze(1).broadcast_to(shape),
                                    prio[:, 2 * g:2 * g + 2, :].rearrange("p i e -> p (i e)").unsqueeze(2)
                                    .broadcast_to(shape), ALU.is_equal).then_inc(s["m_D"], 1)

            def add_mixture(f):
                dve.wait_ge(s["m_comb"], f + 1)
                xo = sl(X, f).rearrange("p o i d -> p (o i d)")
                v.tensor_tensor(xo, xo, HBK[:], ALU.add).then_inc(s["m_out"], 1)

            def step0(a, f, layer=0):
                A, M = a is not None, f is not None
                if A:
                    a_norm(a, layer)
                if M:
                    f_norm(f, 0)
                if A:
                    scale_q(a, layer)
                if M:
                    st = Steps("m_route", ROUTE0 * f)
                    route0(f, st)
                if A:
                    softmax_shift(a, 0, layer)
                if M:
                    slots(f, st)
                    assert st.n == ROUTE0
                if A:
                    softmax_shift(a, 1, layer)
                    normalise(a, 0)
                    softmax_shift(a, 2, layer)
                    add_residual(a, 0, layer)
                    normalise(a, 1)
                    softmax_shift(a, 3, layer)
                    add_residual(a, 1, layer)
                    normalise(a, 2)
                    add_residual(a, 2, layer)
                    normalise(a, 3)
                if M:
                    add_mixture(f)
                if A:
                    add_residual(a, 3, layer)

            def route1(f):
                m = f - B
                st = Steps("n_route", ROUTE1 * m)
                dve.wait_ge(s["n_logits"], m + 1)
                nb = [P, NT, NG]
                st(v.tensor_tensor(r_p2[:], EBK[:, 0:NT * NG].rearrange("p (i e) -> p i e", i=NT),
                                   gb_s[:].unsqueeze(1).broadcast_to(nb), ALU.add))
                top2(st, NG, oh1[:, :, 0, :], oh1[:, :, 1, :], 0, r_p2[:], "n_exp", m)
                st(v.tensor_tensor(r_q[:], oh1[:, :, 0, :], oh1[:, :, 1, :], ALU.add))
                st(v.tensor_tensor(cw[:], r_p[:, :, 0:NE], r_q[:, :, 0:NE], ALU.mult))
                st(v.tensor_reduce(r_s[:], cw[:], AX.X, ALU.add))
                st(v.tensor_scalar(r_m[:], r_s[:], 0.0, None, ALU.is_le))
                st(v.tensor_tensor(r_s[:], r_s[:], r_m[:], ALU.add))
                st(v.reciprocal(r_r[:], r_s[:]))
                st(v.tensor_tensor(cw[:], cw[:], r_r[:].unsqueeze(2).broadcast_to([P, NT, NE]), ALU.mult))
                assert st.n == ROUTE1

            def start_acc(f):
                m = f - B
                dve.wait_ge(s["n_bias"], m + 1)
                xo = sl(X, m).rearrange("p o i d -> p (o i d)")
                if not static_first(m):
                    dve.wait_ge(s["st_out"], 16 * m)
                v.tensor_tensor(acc[:].rearrange("p i d -> p (i d)"), EBK[:], xo, ALU.add).then_inc(s["n_acc"], 1)
                dve.wait_ge(s["n_acc"], m + 1)

            def weigh_experts(f, i):
                m = f - B
                for e in range(NE):
                    n = e // 4
                    if e % 4 == 0:
                        dve.wait_ge(s["n_eo"], 2 * NT * m + 2 * i + n + 1)
                    ins = v.scalar_tensor_tensor(acc[:, i, :], [HBK, EBK][n][:, (e % 4) * D:(e % 4 + 1) * D],
                                                 cw[:, i, e:e + 1], acc[:, i, :], ALU.mult, ALU.add)
                    if e % 4 == 3:
                        ins.then_inc(s["n_used"], 1)
                        dve.wait_ge(s["n_used"], 2 * NT * m + 2 * i + n + 1)
                    else:
                        ins.then_inc(s["n_sum"], 1)
                        dve.wait_ge(s["n_sum"], 6 * (NT * m + i) + 3 * n + e % 4 + 1)

            def step1(a, f):
                A, M = a is not None, f is not None
                if A:
                    a_norm(a, 1)
                if M:
                    f_norm(f, 1)
                if A:
                    scale_q(a, 1)
                if M:
                    route1(f)
                if A:
                    softmax_shift(a, 0, 1)
                    softmax_shift(a, 1, 1)
                    normalise(a, 0)
                if M:
                    start_acc(f)
                    weigh_experts(f, 0)
                if A:
                    softmax_shift(a, 2, 1)
                    add_residual(a, 0, 1)
                    normalise(a, 1)
                if M:
                    weigh_experts(f, 1)
                if A:
                    softmax_shift(a, 3, 1)
                    add_residual(a, 1, 1)
                    normalise(a, 2)
                if M:
                    weigh_experts(f, 2)
                if A:
                    add_residual(a, 2, 1)
                    normalise(a, 3)
                if M:
                    weigh_experts(f, 3)
                if A:
                    add_residual(a, 3, 1)

            step0(0, None)
            step0(1, 0)
            with dve.Fori(1, B - 1) as n:
                step0(n + 1, n)
            step0(B, B - 1, layer=1)
            step1(B + 1, B)
            with dve.Fori(1, B - 1) as n:
                step1(n + B + 1, n + B)
            step1(None, 2 * B - 1)


_INS = ['x', 'ctx_1024', 'fside_Bx16xSxS2_0', 'fside_SxS2_0', 'mask_BxSxS2_ik1', 'mask_BxS2_bf0',
        'L0_xattn_Wq', 'L0_xattn_bq', 'L0_xattn_Wk', 'L0_xattn_bk', 'L0_xattn_Wv', 'L0_xattn_bv',
        'L0_xattn_Wo', 'L0_xattn_bo', 'L0_ffn_w_router', 'L0_ffn_wi', 'L0_ffn_wo',
        'L1_xattn_Wq', 'L1_xattn_bq', 'L1_xattn_Wk', 'L1_xattn_bk', 'L1_xattn_Wv', 'L1_xattn_bv',
        'L1_xattn_Wo', 'L1_xattn_bo', 'L1_ffn_gate_w', 'L1_ffn_gate_b', 'L1_ffn_expert_w', 'L1_ffn_expert_b']


def kernel(**inputs):
    import numpy as _np
    import concourse.bacc as _bacc
    from concourse import mybir as _mybir
    from concourse.bass_utils import run_bass_kernel_spmd as _run

    nc = _bacc.Bacc("TRN2", target_bir_lowering=False, num_devices=1)
    arrays, t = {}, {}
    for name in _INS:
        a = _np.ascontiguousarray(inputs[name])
        if a.dtype == _np.bool_:
            a = a.reshape(-1).view(_np.int32)
        arrays[f"in_{name}"] = a
        t[name] = nc.dram_tensor(f"in_{name}", a.shape, _mybir.dt.from_np(a.dtype), kind="ExternalInput").ap()
    out = nc.dram_tensor("out", inputs["x"].shape, _mybir.dt.float32, kind="ExternalOutput").ap()
    heads = [[t[f"L{n}_xattn_{k}{m}"] for m in "qkvo"] for n in range(2) for k in "Wb"]
    bass_xattn_moe_twice(
        nc, t['x'], t['ctx_1024'], t['fside_Bx16xSxS2_0'], t['fside_SxS2_0'], t['mask_BxSxS2_ik1'],
        t['mask_BxS2_bf0'], heads[0], heads[1], t['L0_ffn_w_router'], t['L0_ffn_wi'], t['L0_ffn_wo'],
        heads[2], heads[3], t['L1_ffn_gate_w'], t['L1_ffn_gate_b'], t['L1_ffn_expert_w'],
        t['L1_ffn_expert_b'], out)
    r = _run(nc, [arrays], core_ids=[0])
    return r.results[0]["out"]
```

```python
from contextlib import ExitStack

import concourse.bass as bass
from concourse import mybir

F32 = mybir.dt.float32
BF16 = mybir.dt.bfloat16
I32 = mybir.dt.int32
U8 = mybir.dt.uint8
ALU = mybir.AluOpType
ACT = mybir.ActivationFunctionType
AX = mybir.AxisListType

P = 128


def bass_xattn_moe_twice(nc, x, ctx_in, bias, attn_mask, mask, pad_mask,
                         w0, b0, w_router, wi, wo, w1, b1, gate_w, gate_b, expert_w, expert_b, out):
    B, S, D = x.shape
    H, J = bias.shape[1], bias.shape[3]
    DK = D // H
    NE, _, F = wi.shape
    NG = gate_w.shape[0]
    CAP = 64
    NT = S // P
    FC = F // P
    HJ = H * J
    NC = -(-HJ // P)
    HJP = NC * P
    HB = 512 // J
    BANKS = [(0, HB), (HB, 2 * HB), (2 * HB, H)]
    HQ = 32 // DK
    BLOCKS = [(q, c) for q in range(4) for c in range(NC)
              if P * c < J * HQ * (q + 1) and P * (c + 1) > J * HQ * q]
    NB = len(BLOCKS)
    VSPLIT = 7
    ROUNDS = [[k for k, (q, c) in enumerate(BLOCKS) if c - [b[1] for b in BLOCKS if b[0] == q][0] == n]
              for n in range(4)]
    SCALE = float(DK) ** -0.5
    EPS = 1e-5
    MASKED = -1e30
    LAYERS = 2
    ROUTE0, ROUTE1 = 18, 24

    ctx = ExitStack()
    with ctx:
        def sb(name, shape, dt=F32):
            return ctx.enter_context(nc.sbuf_tensor(name, shape, dt))

        def bank(name, shape):
            return ctx.enter_context(nc.psum_tensor(name, shape, F32))

        def sem(name):
            return ctx.enter_context(nc.semaphore(name))

        X = sb("X", [P, B, NT, D])
        ident = sb("ident", [P, P])
        incl = sb("incl", [P, P], BF16)
        strict = sb("strict", [P, P], BF16)
        ones = sb("ones", [P, P], BF16)
        iota1 = sb("iota1", [P, CAP])
        rank = sb("rank", [P, NG])
        half = sb("half", [P, NT])
        headmask = sb("headmask", [P, H])
        rowmask = sb("rowmask", [P, NB, HQ, DK])
        identb = sb("identb", [P, P], BF16)
        W = sb("W", [P, 8, D])
        WT = sb("WT", [P, 8, D])
        bcol = sb("bcol", [P, 6])
        bo = sb("bo", [P, LAYERS, D])
        ctxn = sb("ctxn", [J, B, D])
        ctxT = sb("ctxT", [P, B, J])
        ctxR = sb("ctxR", [P, HJP])
        kT = sb("kT", [P, LAYERS, B, J])
        KB = sb("KB", [P, 2 * B, HJ])
        VB = sb("VB", [P, 2 * B, NB, 32])
        vals = sb("vals", [P, NB, HQ, DK])
        am = sb("am", [P, NT, J])
        padw = sb("padw", [P, B * J // 4], I32)
        padb = padw[:].bitcast(U8).rearrange("p (b j) -> p b j", b=B)
        padn = sb("padn", [P, B, J])
        amp = sb("amp", [P, NT, J])
        BI = [sb(f"BI{g}", [P, H, 2, J]) for g in range(2)]
        MI = [sb(f"MI{g}", [P, 2, J], I32) for g in range(2)]
        MN = [sb(f"MN{g}", [P, 2, J], BF16) for g in range(2)]
        wi_s = sb("wi_s", [P, NE, F])
        wo_s = sb("wo_s", [P, NE, FC, D])
        wr_s = sb("wr_s", [P, NE])
        gw_s = sb("gw_s", [NG, D])
        gwT = sb("gwT", [P, NG])
        gb_s = sb("gb_s", [P, NG])
        ew_s = sb("ew_s", [P, NE, D])
        eb_s = sb("eb_s", [NT * NE, NT, D])

        a_st = sb("a_st", [P, NT, 6])
        a_mv = sb("a_mv", [P, NT, 2])
        a_ve = sb("a_ve", [P, NT])
        a_rs = sb("a_rs", [P, NT])
        a_xn = sb("a_xn", [P, NT, D])
        a_xT = sb("a_xT", [P, S])
        qT = sb("qT", [P, S])
        xr = sb("xr", [P, NT, D])
        SC = [sb(f"SC{n}", [P, HJP]) for n in range(2)]
        mx = [sb(f"mx{n}", [P, H]) for n in range(2)]
        PT = sb("PT", [P, NC, P])
        rc = sb("rc", [P, P])
        oT = sb("oT", [P, P])

        f_st = sb("f_st", [P, NT, 6])
        f_mv = sb("f_mv", [P, NT, 2])
        f_ve = sb("f_ve", [P, NT])
        f_rs = sb("f_rs", [P, NT])
        f_xn = sb("f_xn", [P, NT, D])
        f_xT = sb("f_xT", [P, S])
        xh = sb("xh", [P, NT, D], BF16)
        xm = sb("xm", [P, NT, D], BF16)
        xl = sb("xl", [P, NT, D], BF16)
        r_m = sb("r_m", [P, NT])
        r_l = sb("r_l", [P, NT, NG])
        r_e = sb("r_e", [P, NT, NG])
        r_s = sb("r_s", [P, NT])
        r_r = sb("r_r", [P, NT])
        r_p = sb("r_p", [P, NT, NG])
        r_p2 = sb("r_p2", [P, NT, NG])
        r_q = sb("r_q", [P, NT, NG])
        r_k = sb("r_k", [P, NT, NG])
        oh = sb("oh", [P, NT, 2, NE], BF16)
        oh1 = sb("oh1", [P, NT, 2, NG])
        r_c = sb("r_c", [P, NT, 2, NE])
        prio = sb("prio", [P, NT, NE])
        Dm = sb("Dm", [P, NT, NE, CAP], BF16)
        Cm = ctxR[:, 0:2 * NE * CAP].rearrange("p (n e c) -> p n e c", n=2, e=NE)
        CT = sb("CT", [P, NT, NE // 2, P])
        ein = sb("ein", [P, NE, 2, CAP])
        hT = [sb(f"hT{n}", [P, FC, 2, CAP]) for n in range(2)]
        eo = W[:].rearrange("p (k g) d -> p k g d", g=2)
        cw = sb("cw", [P, NT, NE])
        cwT = sb("cwT", [NT * NE, P])
        acc = sb("acc", [P, NT, D])
        xres = acc
        bvb = a_xn[:, 0:LAYERS, :]

        SP3 = bank("SP3", [P, 3, 512])
        TB = [bank(f"TB{n}", [P, 512]) for n in range(2)]
        MB = bank("MB", [P, 512])
        HBK = bank("HBK", [P, 512])
        EBK = bank("EBK", [P, 512])

        names = """ld_ctx ld_x ld_w ld_vec ld_moe ld_am ld_e1 st_out
        c_set c_ok c_idn k_ctxT k_ctxTs k_w k_ws k_kT k_kTs k_rep k_v k_vb k_kb k_pad k_gw k_gws k_eb0 k_eb
        a_stats a_aggr a_veps a_rstd a_xnok a_xTok a_xTs a_qok a_qTs a_xrok k_bvb k_bo k_bos k_idb k_kb1 a_vals
        biasok0 biasok1 maskn ampok
        scores added rawmax rowmax shifted probs trE PTs pv recips normed proj resid
        f_stats f_aggr f_veps f_rstd f_xnok f_xTok f_xTs
        m_logits m_route m_exp m_cum m_split m_D m_C m_disp m_eins m_CT m_CTs m_h m_hs m_eo m_eos m_comb m_out
        n_logits n_route n_exp n_cwT n_cwTs n_bias n_eo n_used n_acc n_sum""".split()
        s = {n: sem(n) for n in names}

        def static_first(run):
            return isinstance(run, int) and run == 0

        def wait_alone(eng, *waits):
            held = [(q, v if isinstance(v, int) else eng.to_reg(v)) for q, v in waits]
            eng.wait_ge(s["c_idn"], 1)
            for q, v in held:
                eng.wait_ge(q, v)

        def sl(t, run):
            return t[:, bass.ds(run, 1)]

        x_v = x.rearrange("b (g p r) d -> b p g r d", g=2, r=2)
        out_v = out.rearrange("b (g p r) d -> b p g r d", g=2, r=2)
        am_v = attn_mask.rearrange("(g p r) j -> p g r j", g=2, r=2)
        bias_v = bias.rearrange("b h (g p r) j -> b g p h (r j)", g=2, r=2)
        mask_v = mask.rearrange("b (g p r) j -> b g p (r j)", g=2, r=2)

        block = ctx.enter_context(nc.Block())

        @block.sync
        def _(sp):
            sp.dma_start(ctxn[:], ctx_in.rearrange("b j d -> j b d")).then_inc(s["ld_ctx"], 16)
            for n in range(4):
                sp.dma_start(W[:, n, :], w0[n]).then_inc(s["ld_w"], 16)
            for n in range(4):
                sp.dma_start(W[:, 4 + n, :], w1[n]).then_inc(s["ld_w"], 16)
            for b in range(B):
                sp.dma_start(X[:, b].rearrange("p (g r) d -> p g r d", g=2), x_v[b]).then_inc(s["ld_x"], 16)

            def load_bias(a):
                for g, ok in enumerate(("biasok0", "biasok1")):
                    if not static_first(a):
                        wait_alone(sp, (s["added"], (a - 1) * 2 * NT + 4 * (g + 1)),
                                   (s["maskn"], (a - 1) * 2 + g + 1))
                    src_b = bias_v[bass.ds(a, 1), g].rearrange("o p h rj -> (o p) h rj")
                    src_m = mask_v[bass.ds(a, 1), g].rearrange("o p rj -> (o p) rj")
                    sp.dma_start(BI[g][:].rearrange("p h r j -> p h (r j)"), src_b).then_inc(s[ok], 16)
                    sp.dma_start(MI[g][:].rearrange("p r j -> p (r j)"), src_m).then_inc(s[ok], 16)

            load_bias(0)
            sp.dma_start(wi_s[:], wi.rearrange("e d f -> d e f")).then_inc(s["ld_moe"], 16)
            sp.dma_start(wo_s[:], wo.rearrange("e (c f) d -> f e c d", c=FC)).then_inc(s["ld_moe"], 16)
            sp.dma_start(wr_s[:], w_router).then_inc(s["ld_moe"], 16)
            sp.dma_start(am[:].rearrange("p (g r) j -> p g r j", g=2), am_v).then_inc(s["ld_am"], 16)
            sp.dma_start(padw[:], pad_mask.partition_broadcast(P)).then_inc(s["ld_am"], 16)
            sp.dma_start(ew_s[:], expert_w.rearrange("e d h -> d e h")).then_inc(s["ld_e1"], 16)
            with sp.Fori(1, B) as a:
                load_bias(a)

            def store(f):
                b = f - B
                wait_alone(sp, (s["n_used"], 2 * NT * (b + 1)))
                sp.dma_start(out_v[bass.ds(b, 1)].rearrange("o p g r d -> (o p) g r d"),
                             acc[:].rearrange("p (g r) d -> p g r d", g=2)).then_inc(s["st_out"], 16)

            store(B)
            with sp.Fori(1, B) as f:
                store(f + B)
            sp.wait_ge(s["st_out"], 16 * B)

        @block.gpsimd
        def _(pool):
            g = nc.gpsimd
            g.memset(ident[:], 0.0).then_inc(s["c_set"], 1)
            pool.wait_ge(s["c_set"], 1)
            g.affine_select(out=ident[:], in_=ident[:], compare_op=ALU.not_equal, fill=1.0, base=0,
                            pattern=[[-1, P]], channel_multiplier=1).then_inc(s["c_idn"], 1)
            n_set = 1
            for t, v in ((headmask, 1.0), (rowmask, 1.0), (ones, 1.0), (incl, 1.0), (strict, 1.0),
                         (half, -0.5), (eb_s, 0.0), (ctxR, 0.0), (identb, 0.0), (SC[0], 0.0), (SC[1], 0.0)):
                g.memset(t[:], v).then_inc(s["c_set"], 1)
                n_set += 1
            g.iota(iota1[:], pattern=[[1, CAP]], base=1, channel_multiplier=0,
                   allow_small_or_imprecise_dtypes=True).then_inc(s["c_ok"], 1)
            g.iota(rank[:], pattern=[[-1, NG]], base=NG, channel_multiplier=0,
                   allow_small_or_imprecise_dtypes=True).then_inc(s["c_ok"], 1)
            pool.wait_ge(s["c_set"], n_set)
            g.affine_select(out=headmask[:], in_=headmask[:], compare_op=ALU.is_ge, fill=0.0, base=0,
                            pattern=[[-DK, H]], channel_multiplier=1).then_inc(s["c_ok"], 1)
            pool.wait_ge(s["c_ok"], 3)
            g.affine_select(out=headmask[:], in_=headmask[:], compare_op=ALU.is_ge, fill=0.0, base=DK - 1,
                            pattern=[[DK, H]], channel_multiplier=-1).then_inc(s["c_ok"], 1)
            g.affine_select(out=incl[:], in_=incl[:], compare_op=ALU.is_ge, fill=0.0, base=0,
                            pattern=[[1, P]], channel_multiplier=-1).then_inc(s["c_ok"], 1)
            g.affine_select(out=strict[:], in_=strict[:], compare_op=ALU.is_ge, fill=0.0, base=-1,
                            pattern=[[1, P]], channel_multiplier=-1).then_inc(s["c_ok"], 1)
            QB = [[k for k in range(NB) if BLOCKS[k][0] == q] for q in range(4)]
            for q in range(4):
                k0, nq, base = QB[q][0], len(QB[q]), P * BLOCKS[QB[q][0]][1] - J * HQ * q
                part = rowmask[:, k0:k0 + nq]
                g.affine_select(out=part, in_=part, compare_op=ALU.is_ge, fill=0.0, base=base,
                                pattern=[[P, nq], [-J, HQ], [0, DK]], channel_multiplier=1).then_inc(s["c_ok"], 1)
            pool.wait_ge(s["c_ok"], 10)
            for q in range(4):
                k0, nq, base = QB[q][0], len(QB[q]), P * BLOCKS[QB[q][0]][1] - J * HQ * q
                part = rowmask[:, k0:k0 + nq]
                g.affine_select(out=part, in_=part, compare_op=ALU.is_ge, fill=0.0, base=J - 1 - base,
                                pattern=[[-P, nq], [J, HQ], [0, DK]], channel_multiplier=-1).then_inc(s["c_ok"], 1)
            g.affine_select(out=identb[:], in_=identb[:], compare_op=ALU.not_equal, fill=1.0, base=0,
                            pattern=[[-1, P]], channel_multiplier=1).then_inc(s["k_idb"], 1)

            for n, v in enumerate((b0[0], b0[1], b0[2], b1[0], b1[1], b1[2])):
                g.dma_start(bcol[:, n:n + 1], v.rearrange("(p o) -> p o", o=1)).then_inc(s["ld_vec"], 16)
            g.dma_start(bo[:, 0, :], b0[3].partition_broadcast(P)).then_inc(s["ld_vec"], 16)
            g.dma_start(bo[:, 1, :], b1[3].partition_broadcast(P)).then_inc(s["ld_vec"], 16)
            g.dma_start(gb_s[:], gate_b.partition_broadcast(P)).then_inc(s["ld_vec"], 16)
            g.dma_start(gw_s[:], gate_w).then_inc(s["ld_vec"], 16)
            for i in range(NT):
                g.dma_start(eb_s[NE * i:NE * (i + 1), i, :], expert_b).then_inc(s["ld_vec"], 16)

            def rstd(aggr, mv, ve, rs, okv, okr, run):
                wait_alone(pool, (s[aggr], NT * (run + 1)))
                g.tensor_scalar(ve[:], mv[:, :, 1], EPS, None, ALU.add).then_inc(s[okv], 1)
                pool.wait_ge(s[okv], run + 1)
                g.tensor_tensor(rs[:], ve[:], half[:], ALU.pow).then_inc(s[okr], 1)

            def a_rstd(a):
                rstd("a_aggr", a_mv, a_ve, a_rs, "a_veps", "a_rstd", a)

            def f_rstd(f):
                rstd("f_aggr", f_mv, f_ve, f_rs, "f_veps", "f_rstd", f)

            def residual_bias(a, layer):
                if layer == 0:
                    pool.wait_ge(s["ld_x"], 16 * B)
                    if static_first(a):
                        pool.wait_ge(s["k_bos"], LAYERS)
                else:
                    pool.wait_ge(s["m_out"], a - B + 1)
                if not static_first(a):
                    pool.wait_ge(s["resid"], NT * a)
                xin = sl(X, a - B * layer).rearrange("p o i d -> p (o i) d")
                g.tensor_tensor(xr[:], xin, bo[:, layer:layer + 1, :].broadcast_to([P, NT, D]),
                                ALU.add).then_inc(s["a_xrok"], 1)

            def mask_out(a):
                for gi in range(2):
                    wait_alone(pool, (s[f"biasok{gi}"], 32 * (a + 1)),
                               *([] if static_first(a) else [(s["scores"], 2 * NT * a)]))
                    g.tensor_scalar(MN[gi][:], MI[gi][:], 0, MASKED, ALU.is_equal, ALU.mult)\
                        .then_inc(s["maskn"], 1)

            def block_keys(a):
                g.tensor_tensor(sl(KB, a + B).rearrange("p o (h j) -> p (o h) j", h=H),
                                kT[:, 1, bass.ds(a, 1), :].broadcast_to([P, H, J]),
                                headmask[:].unsqueeze(2).broadcast_to([P, H, J]), ALU.mult).then_inc(s["k_kb1"], 1)

            def take_values(a):
                if static_first(a):
                    pool.wait_ge(s["k_vb"], 2 * B)
                else:
                    pool.wait_ge(s["pv"], NT * a)
                g.tensor_tensor(vals[:], sl(VB, a).rearrange("p o k (h d) -> p (o k) h d", h=HQ), rowmask[:],
                                ALU.mult).then_inc(s["a_vals"], 1)

            def shift(a, i):
                pool.wait_ge(s["rowmax"], NT * a + i + 1)
                S3 = SC[i % 2][:, 0:HJ].rearrange("p (h j) -> p h j", h=H)
                g.tensor_tensor(S3, S3, mx[i % 2][:].unsqueeze(2).broadcast_to([P, H, J]), ALU.subtract)\
                    .then_inc(s["shifted"], 1)

            def mask_attn(a):
                b = a - B
                if not static_first(b):
                    pool.wait_ge(s["added"], 2 * NT * a)
                g.tensor_tensor(amp[:], am[:], sl(padn, b).broadcast_to([P, NT, J]), ALU.add)\
                    .then_inc(s["ampok"], 1)

            def split_x(f):
                wait_alone(pool, (s["f_xnok"], NT * (f + 1)), *([] if static_first(f) else [(s["m_disp"], 2 * f)]))
                base = 4 * f
                g.tensor_copy(xh[:], f_xn[:]).then_inc(s["m_split"], 1)
                pool.wait_ge(s["m_split"], base + 1)
                g.tensor_tensor(xres[:], f_xn[:], xh[:], ALU.subtract).then_inc(s["m_split"], 1)
                wait_alone(pool, (s["m_split"], base + 2))
                g.tensor_copy(xm[:], xres[:]).then_inc(s["m_split"], 1)
                pool.wait_ge(s["m_split"], base + 3)
                g.tensor_tensor(xl[:], xres[:], xm[:], ALU.subtract).then_inc(s["m_split"], 1)

            def combine_weights(f, i):
                if static_first(f) and i == 0:
                    pool.wait_ge(s["k_v"], B)
                pool.wait_ge(s["m_D"], 2 * f + i // 2 + 1)
                if i >= 2 or not static_first(f):
                    pool.wait_ge(s["m_CT"], NT * f + i - 1)
                g.tensor_tensor(Cm[:, i % 2], Dm[:, i],
                                r_p[:, i, 0:NE].unsqueeze(2).broadcast_to([P, NE, CAP]),
                                ALU.mult).then_inc(s["m_C"], 1)

            def step(a, la, f, lf):
                if a is not None:
                    a_rstd(a)
                if f is not None:
                    f_rstd(f)
                if a is not None:
                    residual_bias(a, la)
                    if la == 0:
                        mask_out(a)
                    else:
                        mask_attn(a)
                    take_values(a)
                    shift(a, 0)
                    shift(a, 1)
                if f is not None and lf == 0:
                    split_x(f)
                    combine_weights(f, 0)
                    combine_weights(f, 1)
                if a is not None:
                    shift(a, 2)
                if f is not None and lf == 0:
                    combine_weights(f, 2)
                    combine_weights(f, 3)
                if a is not None:
                    shift(a, 3)
                    if la == 0:
                        block_keys(a)

            step(0, 0, None, 0)
            step(1, 0, 0, 0)
            with pool.Fori(2, B) as a:
                step(a, 0, a - 1, 0)
            pool.wait_ge(s["ld_am"], 32)
            g.tensor_scalar(padn[:], padb, -3e38, 2.0, ALU.mult, ALU.mult).then_inc(s["k_pad"], 1)
            pool.wait_ge(s["k_pad"], 1)
            step(B, 1, B - 1, 0)
            step(B + 1, 1, B, 1)
            with pool.Fori(2, B) as n:
                step(n + B, 1, n + B - 1, 1)
            step(None, 1, 2 * B - 1, 1)

        @block.scalar
        def _(act):
            sc = nc.scalar
            act.wait_ge(s["k_ctxT"], 1)
            sc.copy(ctxT[:].rearrange("p b j -> p (b j)"), MB[:, 0:B * J]).then_inc(s["k_ctxTs"], 1)
            for n in range(2):
                act.wait_ge(s["k_w"], n + 1)
                sc.copy(WT[:, 4 * n:4 * n + 4, :].rearrange("p n d -> p (n d)"), [HBK, EBK][n][:])\
                    .then_inc(s["k_ws"], 1)
            act.wait_ge(s["ld_vec"], 16 * 14)
            for n in range(2):
                act.wait_ge(s["k_kT"], n + 1)
                sc.activation(kT[:, n].rearrange("p b j -> p (b j)"), SP3[:, n, 0:B * J], ACT.Identity,
                              bias=bcol[:, 3 * n + 1:3 * n + 2]).then_inc(s["k_kTs"], 1)
            act.wait_ge(s["k_gw"], 1)
            sc.copy(gwT[:], SP3[:, 2, 0:NG]).then_inc(s["k_gws"], 1)

            def a_xTcopy(a):
                act.wait_ge(s["a_xTok"], a + 1)
                sc.copy(a_xT[:], MB[:]).then_inc(s["a_xTs"], 1)

            def f_xTcopy(f):
                act.wait_ge(s["f_xTok"], f + 1)
                sc.copy(f_xT[:], MB[:]).then_inc(s["f_xTs"], 1)

            def softmax_exp(a, i):
                act.wait_ge(s["shifted"], NT * a + i + 1)
                sc.activation(SC[i % 2][:, 0:HJ], SC[i % 2][:, 0:HJ], ACT.Exp).then_inc(s["probs"], 1)

            def copy_PT(a, i):
                t = NT * a + i
                for n, (c0, c1) in enumerate(((0, 4), (4, 8), (8, NC))):
                    act.wait_ge(s["trE"], 3 * t + n + 1)
                    if n == 0 and not static_first(a if i == 0 else 1):
                        act.wait_ge(s["pv"], t)
                    sc.copy(PT[:, c0:c1, :].rearrange("p c t -> p (c t)"),
                            TB[n % 2][:, 0:(c1 - c0) * P]).then_inc(s["PTs"], 1)

            def route_exp(route, per, k, ok, ne, run):
                act.wait_ge(s[route], per * run + k)
                sc.activation(r_e[:, :, 0:ne], r_l[:, :, 0:ne], ACT.Exp).then_inc(s[ok], 1)

            def copy_ein(f, g):
                act.wait_ge(s["m_disp"], 2 * f + g + 1)
                sc.copy(ein[:, :, g, :], [HBK, EBK][g][:].rearrange("p (e c) -> p e c", e=NE))\
                    .then_inc(s["m_eins"], 1)

            def copy_CT(f):
                for i in range(NT):
                    act.wait_ge(s["m_CT"], NT * f + i + 1)
                    sc.copy(CT[:, i].rearrange("p k t -> p (k t)"), [HBK, EBK][i % 2][:]).then_inc(s["m_CTs"], 1)

            def gelu(f, e):
                act.wait_ge(s["m_h"], NE * f + e + 1)
                sc.activation(hT[e % 2][:].rearrange("p c g s -> p (c g s)"), HBK[:], ACT.Gelu_apprx_tanh)\
                    .then_inc(s["m_hs"], 1)

            def copy_eo(f, k):
                act.wait_ge(s["m_eo"], NE // 2 * f + k + 1)
                sc.copy(eo[:, k].rearrange("p g d -> p (g d)"), EBK[:, 0:2 * D]).then_inc(s["m_eos"], 1)

            def copy_cwT(f):
                act.wait_ge(s["n_cwT"], f - B + 1)
                sc.copy(cwT[:], EBK[0:NT * NE, 0:P]).then_inc(s["n_cwTs"], 1)

            def step(a, la, f, lf, t):
                A, M, T = a is not None, f is not None, t is not None
                if T:
                    gelu(t, 4)
                    gelu(t, 5)
                if A:
                    a_xTcopy(a)
                if T:
                    gelu(t, 6)
                    copy_eo(t, 2)
                    gelu(t, 7)
                    copy_eo(t, 3)
                if M:
                    f_xTcopy(f)
                if A:
                    softmax_exp(a, 0)
                if M and lf == 0:
                    route_exp("m_route", ROUTE0, 2, "m_exp", NE, f)
                if M and lf == 1:
                    route_exp("n_route", ROUTE1, 3, "n_exp", NG, f - B)
                if A:
                    copy_PT(a, 0)
                    softmax_exp(a, 1)
                if M and lf == 1:
                    copy_cwT(f)
                if M and lf == 0:
                    copy_ein(f, 0)
                if A:
                    copy_PT(a, 1)
                if M and lf == 0:
                    copy_ein(f, 1)
                    copy_CT(f)
                if A:
                    softmax_exp(a, 2)
                    copy_PT(a, 2)
                    softmax_exp(a, 3)
                if M and lf == 0:
                    gelu(f, 0)
                if A:
                    copy_PT(a, 3)
                if M and lf == 0:
                    gelu(f, 1)
                    gelu(f, 2)
                    copy_eo(f, 0)
                    gelu(f, 3)
                    copy_eo(f, 1)

            step(0, 0, None, 0, None)
            step(1, 0, 0, 0, None)
            with act.Fori(2, B) as a:
                step(a, 0, a - 1, 0, a - 2)
            step(B, 1, B - 1, 0, B - 2)
            step(B + 1, 1, B, 1, B - 1)
            with act.Fori(2, B) as n:
                step(n + B, 1, n + B - 1, 1, None)
            step(None, 1, 2 * B - 1, 1, None)

        @block.tensor
        def _(pe):
            te = nc.tensor
            pe.wait_ge(s["c_idn"], 1)
            pe.wait_ge(s["ld_ctx"], 16)
            for b in range(B):
                last = te.transpose(MB[:, b * J:(b + 1) * J], ctxn[:, b, :], ident[0:J, 0:J])
            last.then_inc(s["k_ctxT"], 1)
            pe.wait_ge(s["ld_w"], 16 * 8)
            for n in range(8):
                last = te.transpose([HBK, EBK][n // 4][:, (n % 4) * D:(n % 4 + 1) * D], W[:, n, :], ident[:])
                if n % 4 == 3:
                    last.then_inc(s["k_w"], 1)
            pe.wait_ge(s["k_ctxTs"], 1)
            pe.wait_ge(s["k_ws"], 2)
            for n in range(2):
                te.matmul(SP3[:, n, 0:B * J], WT[:, 4 * n + 1, :], ctxT[:].rearrange("p b j -> p (b j)"),
                          start=True, stop=True).then_inc(s["k_kT"], 1)
            pe.wait_ge(s["ld_vec"], 16 * 14)
            te.transpose(SP3[:, 2, 0:NG], gw_s[:], ident[0:NG, 0:NG]).then_inc(s["k_gw"], 1)
            pe.wait_ge(s["k_bvb"], LAYERS)
            for n in range(LAYERS):
                te.matmul(MB[:, n * D:(n + 1) * D], bvb[:, n, :], WT[:, 4 * n + 3, :], start=True, stop=True)\
                    .then_inc(s["k_bo"], 1)

            def values(b):
                pe.wait_ge(s["k_rep"], b + 1)
                if not static_first(b):
                    pe.wait_ge(s["k_vb"], 2 * b)
                else:
                    pe.wait_ge(s["k_gws"], 1)
                wv = WT[:].rearrange("p (l m) d -> p l m d", l=LAYERS)[:, :, 2, :]
                for c in range(NC):
                    ks = [k for k in range(NB) if BLOCKS[k][1] == c]
                    n, k0, q0 = ks[0] // VSPLIT, ks[0] % VSPLIT, BLOCKS[ks[0]][0]
                    o = TB[n][:, 64 * k0:64 * (k0 + len(ks))].rearrange("p (k l x) -> p l k x", l=LAYERS, x=32)
                    last = te.matmul(o, ctxR[:, c * P:(c + 1) * P],
                                     wv[:, :, 32 * q0:32 * (q0 + len(ks))].rearrange("p l (k x) -> p l k x", x=32),
                                     start=True, stop=True)
                last.then_inc(s["k_v"], 1)

            values(0)
            with pe.Fori(1, B) as b:
                values(b)
            pe.wait_ge(s["k_vb"], 2 * B)
            pe.wait_ge(s["k_bos"], LAYERS)
            pe.wait_ge(s["k_idb"], 1)

            def a_xTr(a):
                for i in range(NT):
                    pe.wait_ge(s["a_xnok"], NT * a + i + 1)
                    if i == 0 and not static_first(a):
                        pe.wait_ge(s["resid"], NT * a)
                    last = te.transpose(MB[:, i * P:(i + 1) * P], a_xn[:, i, :], ident[:])
                last.then_inc(s["a_xTok"], 1)

            def query(a, layer):
                pe.wait_ge(s["a_xTs"], a + 1)
                te.matmul(MB[:], WT[:, 4 * layer, :], a_xT[:], start=True, stop=True).then_inc(s["a_qok"], 1)

            def attn_scores(a, i, layer):
                t = NT * a + i
                g, r = i // 2, i % 2
                if i == 0:
                    pe.wait_ge(s["a_qTs"], a + 1)
                    if layer == 1:
                        pe.wait_ge(s["k_kb1"], a - B + 1)
                if layer == 0 and r == 0:
                    pe.wait_ge(s["maskn"], 2 * a + g + 1)
                kb = sl(KB, a).rearrange("p o n -> p (o n)")
                for n, (h0, h1) in enumerate(BANKS):
                    if n != 1 and not static_first(a if i == 0 else 1):
                        pe.wait_ge(s["added"], 2 * (t - 1) + (1 if n == 0 else 2))
                    last = te.matmul(SP3[:, n, 0:(h1 - h0) * J], qT[:, i * P:(i + 1) * P],
                                     kb[:, h0 * J:h1 * J], start=True, stop=(layer == 1))
                    if layer == 0:
                        last = te.matmul(SP3[:, n, 0:(h1 - h0) * J], identb[:],
                                         MN[g][:, r:r + 1, :].broadcast_to([P, h1 - h0, J]),
                                         start=False, stop=True)
                    if n > 0:
                        last.then_inc(s["scores"], 1)

            def turn_probs(a, i, n, c0, c1):
                t = NT * a + i
                if n == 0:
                    pe.wait_ge(s["probs"], t + 1)
                if n == 0 and not static_first(a if i == 0 else 1):
                    pe.wait_ge(s["PTs"], 3 * t)
                if n == 2:
                    pe.wait_ge(s["PTs"], 3 * t + 1)
                for c in range(c0, c1):
                    last = te.transpose(TB[n % 2][:, (c - c0) * P:(c - c0 + 1) * P],
                                        SC[i % 2][:, c * P:(c + 1) * P], ident[:])
                last.then_inc(s["trE"], 1)

            def weigh_values(a, i, free):
                t = NT * a + i
                if i == 0:
                    pe.wait_ge(s["a_vals"], a + 1)
                pe.wait_ge(s["PTs"], 3 * t + 3)
                pe.wait_ge(*free)
                for m in range(2):
                    for n, ks in enumerate(ROUNDS):
                        for k in ks:
                            q, c = BLOCKS[k]
                            mine = [j for j in range(NB) if BLOCKS[j][0] == q]
                            w = (vals, rowmask)[m][:, k].rearrange("p h d -> p (h d)")
                            last = te.matmul(MB[32 * q:32 * (q + 1), m * P:(m + 1) * P], w, PT[:, c, :],
                                             start=(k == mine[0]), stop=(k == mine[-1]))
                last.then_inc(s["pv"], 1)

            def project(a, i, layer):
                pe.wait_ge(s["normed"], NT * a + i + 1)
                te.matmul(MB[:, 0:D], oT[:], WT[:, 4 * layer + 3, :], start=True, stop=True)\
                    .then_inc(s["proj"], 1)

            def turn(a, i):
                turn_probs(a, i, 0, 0, 4)
                turn_probs(a, i, 1, 4, 8)
                turn_probs(a, i, 2, 8, NC)

            def f_xTr(f, free):
                for i in range(NT):
                    pe.wait_ge(s["f_xnok"], NT * f + i + 1)
                    if i == 0:
                        pe.wait_ge(*free)
                    last = te.transpose(MB[:, i * P:(i + 1) * P], f_xn[:, i, :], ident[:])
                last.then_inc(s["f_xTok"], 1)

            def logits0(f):
                pe.wait_ge(s["f_xTs"], f + 1)
                if static_first(f):
                    pe.wait_ge(s["ld_moe"], 48)
                for i in range(NT):
                    last = te.matmul(MB[:, i * NE:(i + 1) * NE], f_xT[:, i * P:(i + 1) * P], wr_s[:],
                                     start=True, stop=True)
                last.then_inc(s["m_logits"], 1)

            def positions(f):
                pe.wait_ge(s["m_route"], ROUTE0 * f + 16)
                if not static_first(f):
                    pe.wait_ge(s["m_eos"], NE // 2 * f)
                for g in range(2):
                    t0, t1 = 2 * g, 2 * g + 1
                    for i, first in ((t0, incl), (t1, incl)):
                        o = EBK[:, i * 2 * NE:(i + 1) * 2 * NE]
                        second = strict if i == t0 else incl
                        te.matmul(o, first[:], oh[:, t0].rearrange("p k e -> p (k e)"),
                                  start=True, stop=False, skip_group_check=True)
                        te.matmul(o, second[:], oh[:, t1].rearrange("p k e -> p (k e)"),
                                  start=False, stop=False, skip_group_check=True)
                        te.matmul(o[:, NE:], ones[:], oh[:, t0, 0, :], start=False, stop=False,
                                  skip_group_check=True)
                        last = te.matmul(o[:, NE:], ones[:], oh[:, t1, 0, :], start=False, stop=True,
                                         skip_group_check=True)
                last.then_inc(s["m_cum"], 1)

            def dispatch(f, g):
                pe.wait_ge(s["m_split"], 4 * f + 4)
                if g == 0 and not static_first(f):
                    pe.wait_ge(s["m_out"], f)
                pe.wait_ge(s["m_D"], 2 * f + g + 1)
                n = 0
                for i in (2 * g, 2 * g + 1):
                    for part in (xh, xm, xl):
                        last = te.matmul([HBK, EBK][g][:], part[:, i, :], Dm[:, i].rearrange("p e c -> p (e c)"),
                                         start=(n == 0), stop=(n == 5))
                        n += 1
                last.then_inc(s["m_disp"], 1)

            def turn_C(f, i0, i1):
                for i in range(i0, i1):
                    pe.wait_ge(s["m_C"], NT * f + i + 1)
                    if i < 2:
                        pe.wait_ge(s["m_eins"], 2 * f + i + 1)
                    else:
                        pe.wait_ge(s["m_CTs"], NT * f + i - 1)
                    for k in range(NE // 2):
                        last = te.transpose([HBK, EBK][i % 2][:, k * P:(k + 1) * P],
                                            Cm[:, i % 2, 2 * k:2 * k + 2, :].rearrange("p e c -> p (e c)"), ident[:])
                    last.then_inc(s["m_CT"], 1)

            def up(f, e):
                if e == 0:
                    pe.wait_ge(s["m_CTs"], NT * f + NT)
                else:
                    pe.wait_ge(s["m_hs"], NE * f + e)
                for c in range(FC):
                    last = te.matmul(HBK[:, c * P:(c + 1) * P], wi_s[:, e, c * P:(c + 1) * P],
                                     ein[:, e].rearrange("p g c -> p (g c)"), start=True, stop=True)
                last.then_inc(s["m_h"], 1)

            def down(f, k):
                pe.wait_ge(s["m_hs"], NE * f + 2 * k + 2)
                if k > 0:
                    pe.wait_ge(s["m_eos"], NE // 2 * f + k)
                for g in range(2):
                    for c in range(FC):
                        for q in range(2):
                            last = te.matmul(EBK[q * CAP:(q + 1) * CAP, g * D:(g + 1) * D], hT[q][:, c, g, :],
                                             wo_s[:, 2 * k + q, c, :], start=(c == 0), stop=(c == FC - 1))
                last.then_inc(s["m_eo"], 1)

            def combine(f, n):
                pe.wait_ge(s["m_eos"], NE // 2 * (f + 1))
                for i in (2 * n, 2 * n + 1):
                    for k in range(NE // 2):
                        last = te.matmul(HBK[:, i * D:(i + 1) * D], CT[:, i, k, :], eo[:, k, i // 2, :],
                                         start=(k == 0), stop=(k == NE // 2 - 1))
                if n == 1:
                    last.then_inc(s["m_comb"], 1)

            def logits1(f):
                pe.wait_ge(s["f_xTs"], f + 1)
                if static_first(f - B):
                    pe.wait_ge(s["k_gws"], 1)
                    pe.wait_ge(s["ld_e1"], 16)
                for i in range(NT):
                    last = te.matmul(MB[:, i * NG:(i + 1) * NG], f_xT[:, i * P:(i + 1) * P], gwT[:],
                                     start=True, stop=True)
                last.then_inc(s["n_logits"], 1)

            def expert_bias(f):
                m = f - B
                pe.wait_ge(s["n_route"], ROUTE1 * (m + 1))
                if static_first(m):
                    pe.wait_ge(s["m_eos"], NE // 2 * B)
                else:
                    pe.wait_ge(s["n_used"], 2 * NT * m)
                te.transpose(EBK[0:NT * NE, 0:P], cw[:].rearrange("p i e -> p (i e)"), ident[:])\
                    .then_inc(s["n_cwT"], 1)
                pe.wait_ge(s["n_cwTs"], m + 1)
                te.matmul(EBK[:], cwT[:], eb_s[:].rearrange("k i d -> k (i d)"), start=True, stop=True)\
                    .then_inc(s["n_bias"], 1)

            def experts(f, i):
                m = f - B
                for n in range(2):
                    if i == 0:
                        pe.wait_ge(s["n_acc"], m + 1)
                        if static_first(m):
                            pe.wait_ge(s["m_out"], B)
                        else:
                            pe.wait_ge(s["n_used"], 2 * NT * m)
                    else:
                        pe.wait_ge(s["n_used"], 2 * NT * m + 2 * (i - 1) + n + 1)
                    te.matmul([HBK, EBK][n][:], f_xT[:, i * P:(i + 1) * P],
                              ew_s[:, 4 * n:4 * n + 4, :].rearrange("p e d -> p (e d)"),
                              start=True, stop=True).then_inc(s["n_eo"], 1)

            def step(a, la, f, lf, t):
                A, M, T = a is not None, f is not None, t is not None
                M0, M1 = M and lf == 0, M and lf == 1
                if T:
                    up(t, 4)
                    up(t, 5)
                if M:
                    project(f, NT - 1, 0 if isinstance(f, int) and f < B or lf == 0 else 1)
                if A:
                    a_xTr(a)
                if T:
                    down(t, 2)
                if A:
                    query(a, la)
                if T:
                    up(t, 6)
                if A:
                    attn_scores(a, 0, la)
                if T:
                    up(t, 7)
                    down(t, 3)
                if M:
                    f_xTr(f, (s["a_qTs"], a + 1) if A else (s["resid"], NT * 2 * B))
                if T:
                    combine(t, 0)
                if M0:
                    logits0(f)
                if M1:
                    logits1(f)
                if T:
                    combine(t, 1)
                if A:
                    attn_scores(a, 1, la)
                    turn(a, 0)
                    weigh_values(a, 0, (s["m_route"], ROUTE0 * f + 2) if M0 else
                                 (s["n_route"], ROUTE1 * (f - B) + 1) if M1 else (s["a_qTs"], a + 1))
                if M0:
                    positions(f)
                if M1:
                    expert_bias(f)
                if A:
                    attn_scores(a, 2, la)
                if M0:
                    dispatch(f, 0)
                if M1:
                    experts(f, 0)
                if A:
                    turn(a, 1)
                    project(a, 0, la)
                if M0:
                    dispatch(f, 1)
                if M1:
                    experts(f, 1)
                if A:
                    weigh_values(a, 1, (s["resid"], NT * a + 1))
                if M0:
                    turn_C(f, 0, 4)
                if A:
                    attn_scores(a, 3, la)
                    turn(a, 2)
                    project(a, 1, la)
                if M1:
                    experts(f, 2)
                if M0:
                    up(f, 0)
                if A:
                    weigh_values(a, 2, (s["resid"], NT * a + 2))
                    turn(a, 3)
                    project(a, 2, la)
                if M1:
                    experts(f, 3)
                if M0:
                    up(f, 1)
                    down(f, 0)
                if A:
                    weigh_values(a, 3, (s["resid"], NT * a + 3))
                if M0:
                    up(f, 2)
                    up(f, 3)
                    down(f, 1)

            step(0, 0, None, 0, None)
            step(1, 0, 0, 0, None)
            with pe.Fori(2, B) as a:
                step(a, 0, a - 1, 0, a - 2)
            step(B, 1, B - 1, 0, B - 2)
            step(B + 1, 1, B, 1, B - 1)
            with pe.Fori(2, B) as n:
                step(n + B, 1, n + B - 1, 1, None)
            step(None, 1, 2 * B - 1, 1, None)

        @block.vector
        def _(dve):
            v = nc.vector
            dve.wait_ge(s["c_ok"], 14)

            def block_kv(b):
                if static_first(b):
                    dve.wait_ge(s["k_ctxTs"], 1)
                else:
                    dve.wait_ge(s["k_v"], b)
                v.tensor_copy(ctxR[:, 0:HJ].rearrange("p (h j) -> p h j", h=H),
                              sl(ctxT, b).broadcast_to([P, H, J])).then_inc(s["k_rep"], 1)
                if static_first(b):
                    dve.wait_ge(s["k_kTs"], 2)
                v.tensor_tensor(sl(KB, b).rearrange("p o (h j) -> p (o h) j", h=H),
                                kT[:, 0, bass.ds(b, 1), :].broadcast_to([P, H, J]),
                                headmask[:].unsqueeze(2).broadcast_to([P, H, J]), ALU.mult)\
                    .then_inc(s["k_kb"], 1)
                dve.wait_ge(s["k_v"], b + 1)
                for n, (k0, k1) in enumerate(((0, VSPLIT), (VSPLIT, NB))):
                    for l in range(LAYERS):
                        vb = sl(VB, b + l * B).rearrange("p o k v -> p (o k) v")[:, k0:k1, :]
                        ins = v.tensor_tensor(
                            vb, TB[n][:, 0:64 * (k1 - k0)].rearrange("p (k l x) -> p l k x", l=LAYERS, x=32)[:, l],
                            rowmask[:, k0:k1].rearrange("p k h d -> p k (h d)"), ALU.mult)
                    ins.then_inc(s["k_vb"], 1)

            dve.wait_ge(s["ld_vec"], 16 * 14)
            for n in range(LAYERS):
                v.tensor_copy(bvb[:, n, :], bcol[:, 3 * n + 2:3 * n + 3].broadcast_to([P, P])).then_inc(s["k_bvb"], 1)
            dve.wait_ge(s["k_bo"], LAYERS)
            for n in range(LAYERS):
                v.tensor_tensor(bo[:, n, :], bo[:, n, :], MB[:, n * D:(n + 1) * D], ALU.add).then_inc(s["k_bos"], 1)
            block_kv(0)
            with dve.Fori(1, B) as b:
                block_kv(b)
            dve.wait_ge(s["k_kb"], B)
            dve.wait_ge(s["k_vb"], 2 * B)

            def layer_norm(pre, st, mv, rs, xn, run, b, freed, split=None):
                xin = sl(X, b).rearrange("p o i d -> p (o i) d")
                for i in range(NT):
                    v.bn_stats(st[:, i, :], xin[:, i, :]).then_inc(s[pre + "_stats"], 1)
                for i in range(NT):
                    wait_alone(dve, (s[pre + "_stats"], NT * run + i + 1))
                    v.bn_aggr(mv[:, i, :], st[:, i, :]).then_inc(s[pre + "_aggr"], 1)
                if not static_first(run):
                    dve.wait_ge(s[freed], run)
                    if split is not None:
                        dve.wait_ge(s["m_split"], split)
                dve.wait_ge(s[pre + "_rstd"], run + 1)
                for i in range(NT):
                    v.tensor_scalar(xn[:, i, :], xin[:, i, :], mv[:, i, 0:1], rs[:, i:i + 1],
                                    ALU.subtract, ALU.mult).then_inc(s[pre + "_xnok"], 1)

            def a_norm(a, layer):
                if layer == 0:
                    if static_first(a):
                        dve.wait_ge(s["ld_x"], 16 * B)
                else:
                    dve.wait_ge(s["m_out"], a - B + 1)
                layer_norm("a", a_st, a_mv, a_rs, a_xn, a, a - B * layer, "a_xTok")

            def f_norm(f, layer):
                dve.wait_ge(s["resid"], NT * (f + 1))
                layer_norm("f", f_st, f_mv, f_rs, f_xn, f, f - B * layer, "f_xTok",
                           4 * f if layer == 0 else 4 * B)

            def scale_q(a, layer):
                dve.wait_ge(s["a_qok"], a + 1)
                v.tensor_scalar(qT[:], MB[:], bcol[:, 3 * layer:3 * layer + 1], SCALE, ALU.add, ALU.mult)\
                    .then_inc(s["a_qTs"], 1)

            def softmax_max(a, i, layer):
                t = NT * a + i
                g, r = i // 2, i % 2
                S_ = SC[i % 2]
                if layer == 0 and r == 0:
                    dve.wait_ge(s[f"biasok{g}"], 32 * (a + 1))
                if layer == 1 and i == 0:
                    dve.wait_ge(s["ampok"], a - B + 1)
                if not static_first(a) or i >= 2:
                    dve.wait_ge(s["trE"], 3 * (t - 1))
                for n, (h0, h1, k) in enumerate(((0, 2 * HB, 2), (2 * HB, H, 1))):
                    dve.wait_ge(s["scores"], 2 * t + n + 1)
                    hh = (h1 - h0) // k
                    shape = [P, k, hh, J]
                    o = S_[:, h0 * J:h1 * J].rearrange("p (k h j) -> p k h j", k=k, h=hh)
                    i0 = SP3[:, 2 * n:2 * n + k, 0:hh * J].rearrange("p k (h j) -> p k h j", h=hh)
                    if layer == 0:
                        i1 = BI[g][:, h0:h1, r, :].rearrange("p (k h) j -> p k h j", k=k)
                    else:
                        i1 = amp[:, i:i + 1, :].unsqueeze(1).broadcast_to(shape)
                    v.tensor_tensor(o, i0, i1, ALU.add).then_inc(s["added"], 1)
                dve.wait_ge(s["added"], 2 * t + 2)
                S3 = S_[:, 0:HJ].rearrange("p (h j) -> p h j", h=H)
                v.tensor_reduce(mx[i % 2][:], S3, AX.X, ALU.max).then_inc(s["rowmax"], 1)

            def normalise(a, i):
                t = NT * a + i
                dve.wait_ge(s["pv"], t + 1)
                v.reciprocal(rc[:], MB[:, P:2 * P]).then_inc(s["recips"], 1)
                dve.wait_ge(s["recips"], t + 1)
                v.tensor_tensor(oT[:], MB[:, 0:P], rc[:], ALU.mult).then_inc(s["normed"], 1)

            def add_residual(a, i, layer):
                dve.wait_ge(s["proj"], NT * a + i + 1)
                if i == 0:
                    dve.wait_ge(s["a_xrok"], a + 1)
                xo = sl(X, a - B * layer).rearrange("p o i d -> p (o i) d")
                v.tensor_tensor(xo[:, i, :], MB[:, 0:D], xr[:, i, :], ALU.add).then_inc(s["resid"], 1)

            def top2(step, ne, o1, o2, k, lg, exp_ok, run):
                nb = [P, NT, ne]
                l_, e_, p_, p2, q_, k_ = (z[:, :, 0:ne] for z in (r_l, r_e, r_p, r_p2, r_q, r_k))
                rk = rank[:, 0:ne].unsqueeze(1).broadcast_to(nb)
                bc = lambda z: z[:].unsqueeze(2).broadcast_to(nb)
                step(v.tensor_reduce(r_m[:], lg, AX.X, ALU.max))
                step(v.tensor_tensor(l_, lg, bc(r_m), ALU.subtract))
                dve.wait_ge(s[exp_ok], run + 1)
                step(v.tensor_reduce(r_s[:], e_, AX.X, ALU.add))
                step(v.reciprocal(r_r[:], r_s[:]))
                step(v.tensor_tensor(p_, e_, bc(r_r), ALU.mult))
                for n, (src, o) in enumerate(((p_, o1), (p2, o2))):
                    step(v.tensor_reduce(r_m[:], src, AX.X, ALU.max))
                    step(v.tensor_tensor(q_, src, bc(r_m), ALU.is_equal))
                    step(v.tensor_tensor(k_, q_, rk, ALU.mult))
                    step(v.tensor_reduce(r_s[:], k_, AX.X, ALU.max))
                    step(v.tensor_tensor(o, k_, bc(r_s), ALU.is_equal))
                    if n == 0:
                        step(v.scalar_tensor_tensor(p2, o, -2.0, p_, ALU.mult, ALU.add))

            class Steps:

                def __init__(self, name, base):
                    self.name, self.base, self.n = name, base, 0

                def __call__(self, ins):
                    self.n += 1
                    ins.then_inc(s[self.name], 1)
                    dve.wait_ge(s[self.name], self.base + self.n)

            def route0(f, st):
                dve.wait_ge(s["m_logits"], f + 1)
                top2(st, NE, oh[:, :, 0, :], oh[:, :, 1, :], 0,
                     MB[:, 0:NT * NE].rearrange("p (i e) -> p i e", i=NT), "m_exp", f)

            def slots(f, st):
                dve.wait_ge(s["m_cum"], f + 1)
                st(v.tensor_tensor(r_c[:].rearrange("p i k e -> p (i k e)"), EBK[:, 0:NT * 2 * NE],
                                   oh[:].rearrange("p i k e -> p (i k e)"), ALU.mult))
                st(v.tensor_tensor(prio[:], r_c[:, :, 0, :], r_c[:, :, 1, :], ALU.add))
                for g in range(2):
                    shape = [P, 2 * NE, CAP]
                    v.tensor_tensor(Dm[:, 2 * g:2 * g + 2].rearrange("p i e c -> p (i e) c"),
                                    iota1[:].unsqueeze(1).broadcast_to(shape),
                                    prio[:, 2 * g:2 * g + 2, :].rearrange("p i e -> p (i e)").unsqueeze(2)
                                    .broadcast_to(shape), ALU.is_equal).then_inc(s["m_D"], 1)

            def add_mixture(f):
                dve.wait_ge(s["m_comb"], f + 1)
                xo = sl(X, f).rearrange("p o i d -> p (o i d)")
                v.tensor_tensor(xo, xo, HBK[:], ALU.add).then_inc(s["m_out"], 1)

            def route1(f):
                m = f - B
                st = Steps("n_route", ROUTE1 * m)
                dve.wait_ge(s["n_logits"], m + 1)
                nb = [P, NT, NG]
                st(v.tensor_tensor(r_p2[:], MB[:, 0:NT * NG].rearrange("p (i e) -> p i e", i=NT),
                                   gb_s[:].unsqueeze(1).broadcast_to(nb), ALU.add))
                top2(st, NG, oh1[:, :, 0, :], oh1[:, :, 1, :], 0, r_p2[:], "n_exp", m)
                st(v.tensor_tensor(r_q[:], oh1[:, :, 0, :], oh1[:, :, 1, :], ALU.add))
                st(v.tensor_tensor(cw[:], r_p[:, :, 0:NE], r_q[:, :, 0:NE], ALU.mult))
                st(v.tensor_reduce(r_s[:], cw[:], AX.X, ALU.add))
                st(v.tensor_scalar(r_m[:], r_s[:], 0.0, None, ALU.is_le))
                st(v.tensor_tensor(r_s[:], r_s[:], r_m[:], ALU.add))
                st(v.reciprocal(r_r[:], r_s[:]))
                st(v.tensor_tensor(cw[:], cw[:], r_r[:].unsqueeze(2).broadcast_to([P, NT, NE]), ALU.mult))
                assert st.n == ROUTE1

            def start_acc(f):
                m = f - B
                dve.wait_ge(s["n_bias"], m + 1)
                xo = sl(X, m).rearrange("p o i d -> p (o i d)")
                if not static_first(m):
                    dve.wait_ge(s["st_out"], 16 * m)
                v.tensor_tensor(acc[:].rearrange("p i d -> p (i d)"), EBK[:], xo, ALU.add).then_inc(s["n_acc"], 1)
                dve.wait_ge(s["n_acc"], m + 1)

            def weigh_experts(f, i):
                m = f - B
                for e in range(NE):
                    n = e // 4
                    if e % 4 == 0:
                        dve.wait_ge(s["n_eo"], 2 * NT * m + 2 * i + n + 1)
                    ins = v.scalar_tensor_tensor(acc[:, i, :], [HBK, EBK][n][:, (e % 4) * D:(e % 4 + 1) * D],
                                                 cw[:, i, e:e + 1], acc[:, i, :], ALU.mult, ALU.add)
                    if e % 4 == 3:
                        ins.then_inc(s["n_used"], 1)
                        dve.wait_ge(s["n_used"], 2 * NT * m + 2 * i + n + 1)
                    else:
                        ins.then_inc(s["n_sum"], 1)
                        dve.wait_ge(s["n_sum"], 6 * (NT * m + i) + 3 * n + e % 4 + 1)

            def step(a, la, f, lf, t):
                A, M, T = a is not None, f is not None, t is not None
                M0, M1 = M and lf == 0, M and lf == 1
                lp = 0 if isinstance(f, int) and f < B or lf == 0 else 1
                if M:
                    normalise(f, NT - 1)
                if A:
                    a_norm(a, la)
                if M:
                    add_residual(f, NT - 1, lp)
                    f_norm(f, lf)
                if A:
                    scale_q(a, la)
                    softmax_max(a, 0, la)
                if M0:
                    st = Steps("m_route", ROUTE0 * f)
                    route0(f, st)
                if M1:
                    route1(f)
                if T:
                    add_mixture(t)
                if A:
                    softmax_max(a, 1, la)
                    normalise(a, 0)
                if M0:
                    slots(f, st)
                    assert st.n == ROUTE0
                if M1:
                    start_acc(f)
                if A:
                    softmax_max(a, 2, la)
                if M1:
                    weigh_experts(f, 0)
                if A:
                    add_residual(a, 0, la)
                    normalise(a, 1)
                if M1:
                    weigh_experts(f, 1)
                if A:
                    softmax_max(a, 3, la)
                    add_residual(a, 1, la)
                if M1:
                    weigh_experts(f, 2)
                if A:
                    normalise(a, 2)
                    add_residual(a, 2, la)
                if M1:
                    weigh_experts(f, 3)

            step(0, 0, None, 0, None)
            step(1, 0, 0, 0, None)
            with dve.Fori(2, B) as a:
                step(a, 0, a - 1, 0, a - 2)
            step(B, 1, B - 1, 0, B - 2)
            step(B + 1, 1, B, 1, B - 1)
            with dve.Fori(2, B) as n:
                step(n + B, 1, n + B - 1, 1, None)
            step(None, 1, 2 * B - 1, 1, None)


_INS = ['x', 'ctx_1024', 'fside_Bx16xSxS2_0', 'fside_SxS2_0', 'mask_BxSxS2_ik1', 'mask_BxS2_bf0',
        'L0_xattn_Wq', 'L0_xattn_bq', 'L0_xattn_Wk', 'L0_xattn_bk', 'L0_xattn_Wv', 'L0_xattn_bv',
        'L0_xattn_Wo', 'L0_xattn_bo', 'L0_ffn_w_router', 'L0_ffn_wi', 'L0_ffn_wo',
        'L1_xattn_Wq', 'L1_xattn_bq', 'L1_xattn_Wk', 'L1_xattn_bk', 'L1_xattn_Wv', 'L1_xattn_bv',
        'L1_xattn_Wo', 'L1_xattn_bo', 'L1_ffn_gate_w', 'L1_ffn_gate_b', 'L1_ffn_expert_w', 'L1_ffn_expert_b']


def kernel(**inputs):
    import numpy as _np
    import concourse.bacc as _bacc
    from concourse import mybir as _mybir
    from concourse.bass_utils import run_bass_kernel_spmd as _run

    nc = _bacc.Bacc("TRN2", target_bir_lowering=False, num_devices=1)
    arrays, t = {}, {}
    for name in _INS:
        a = _np.ascontiguousarray(inputs[name])
        if a.dtype == _np.bool_:
            a = a.reshape(-1).view(_np.int32)
        arrays[f"in_{name}"] = a
        t[name] = nc.dram_tensor(f"in_{name}", a.shape, _mybir.dt.from_np(a.dtype), kind="ExternalInput").ap()
    out = nc.dram_tensor("out", inputs["x"].shape, _mybir.dt.float32, kind="ExternalOutput").ap()
    heads = [[t[f"L{n}_xattn_{k}{m}"] for m in "qkvo"] for n in range(2) for k in "Wb"]
    bass_xattn_moe_twice(
        nc, t['x'], t['ctx_1024'], t['fside_Bx16xSxS2_0'], t['fside_SxS2_0'], t['mask_BxSxS2_ik1'],
        t['mask_BxS2_bf0'], heads[0], heads[1], t['L0_ffn_w_router'], t['L0_ffn_wi'], t['L0_ffn_wo'],
        heads[2], heads[3], t['L1_ffn_gate_w'], t['L1_ffn_gate_b'], t['L1_ffn_expert_w'],
        t['L1_ffn_expert_b'], out)
    r = _run(nc, [arrays], core_ids=[0])
    return r.results[0]["out"]
```

```python
from contextlib import ExitStack

import concourse.bass as bass
from concourse import mybir

F32 = mybir.dt.float32
BF16 = mybir.dt.bfloat16
I32 = mybir.dt.int32
U8 = mybir.dt.uint8
ALU = mybir.AluOpType
ACT = mybir.ActivationFunctionType
AX = mybir.AxisListType

P = 128


def bass_xattn_moe_twice(nc, x, ctx_in, bias, attn_mask, mask, pad_mask,
                         w0, b0, w_router, wi, wo, w1, b1, gate_w, gate_b, expert_w, expert_b, out):
    B, S, D = x.shape
    H, J = bias.shape[1], bias.shape[3]
    DK = D // H
    NE, _, F = wi.shape
    NG = gate_w.shape[0]
    CAP = 64
    NT = S // P
    FC = F // P
    HJ = H * J
    NC = -(-HJ // P)
    HJP = NC * P
    HB = 512 // J
    BANKS = [(0, HB), (HB, 2 * HB), (2 * HB, H)]
    HQ = 32 // DK
    BLOCKS = [(q, c) for q in range(4) for c in range(NC)
              if P * c < J * HQ * (q + 1) and P * (c + 1) > J * HQ * q]
    NB = len(BLOCKS)
    VSPLIT = 7
    ROUNDS = [[k for k, (q, c) in enumerate(BLOCKS) if c - [b[1] for b in BLOCKS if b[0] == q][0] == n]
              for n in range(4)]
    SCALE = float(DK) ** -0.5
    EPS = 1e-5
    MASKED = -1e30
    LAYERS = 2
    ROUTE0, ROUTE1 = 18, 24

    ctx = ExitStack()
    with ctx:
        def sb(name, shape, dt=F32):
            return ctx.enter_context(nc.sbuf_tensor(name, shape, dt))

        def bank(name, shape):
            return ctx.enter_context(nc.psum_tensor(name, shape, F32))

        def sem(name):
            return ctx.enter_context(nc.semaphore(name))

        X = sb("X", [P, B, NT, D])
        ident = sb("ident", [P, P])
        incl = sb("incl", [P, P], BF16)
        strict = sb("strict", [P, P], BF16)
        ones = sb("ones", [P, P], BF16)
        iota1 = sb("iota1", [P, CAP])
        rank = sb("rank", [P, NG])
        half = sb("half", [P, NT])
        headmask = sb("headmask", [P, H])
        rowmask = sb("rowmask", [P, NB, HQ, DK])
        identb = sb("identb", [P, P], BF16)
        W = sb("W", [P, 8, D])
        WT = sb("WT", [P, 8, D])
        bcol = sb("bcol", [P, 6])
        bo = sb("bo", [P, LAYERS, D])
        ctxn = sb("ctxn", [J, B, D])
        shared = sb("shared", [P, 2 * NE * CAP])
        ctx3 = shared[:, 0:B * 3 * J].rearrange("p (b n j) -> p b n j", b=B, n=3)
        kT = sb("kT", [P, LAYERS, B, J])
        KB = sb("KB", [P, 2 * B, HJ])
        VB = sb("VB", [P, 2 * B, NB, 32])
        vals = sb("vals", [P, NB, HQ, DK])
        am = sb("am", [P, NT, J])
        padw = sb("padw", [P, B * J // 4], I32)
        padb = padw[:].bitcast(U8).rearrange("p (b j) -> p b j", b=B)
        padn = sb("padn", [P, B, J])
        amp = sb("amp", [P, NT, J])
        BI = [sb(f"BI{g}", [P, H, 2, J]) for g in range(2)]
        MI = [sb(f"MI{g}", [P, 2, J], I32) for g in range(2)]
        MN = [sb(f"MN{g}", [P, 2, J], BF16) for g in range(2)]
        wi_s = sb("wi_s", [P, NE, F])
        wo_s = sb("wo_s", [P, NE, FC, D])
        wr_s = sb("wr_s", [P, NE])
        gw_s = sb("gw_s", [NG, D])
        gwT = sb("gwT", [P, NG])
        gb_s = sb("gb_s", [P, NG])
        ew_s = sb("ew_s", [P, NE, D])
        eb_s = sb("eb_s", [NT * NE, NT, D])

        a_st = sb("a_st", [P, NT, 6])
        a_mv = sb("a_mv", [P, NT, 2])
        a_ve = sb("a_ve", [P, NT])
        a_rs = sb("a_rs", [P, NT])
        a_xn = sb("a_xn", [P, NT, D])
        a_xT = sb("a_xT", [P, S])
        qT = sb("qT", [P, S])
        xr = sb("xr", [P, NT, D])
        SC = [sb(f"SC{n}", [P, HJP]) for n in range(2)]
        mx = [sb(f"mx{n}", [P, H]) for n in range(2)]
        PT = sb("PT", [P, NC, P])
        rc = sb("rc", [P, P])
        oT = sb("oT", [P, P])

        f_st = sb("f_st", [P, NT, 6])
        f_mv = sb("f_mv", [P, NT, 2])
        f_ve = sb("f_ve", [P, NT])
        f_rs = sb("f_rs", [P, NT])
        f_xn = sb("f_xn", [P, NT, D])
        f_xT = sb("f_xT", [P, S])
        xh = sb("xh", [P, NT, D], BF16)
        xm = sb("xm", [P, NT, D], BF16)
        xl = sb("xl", [P, NT, D], BF16)
        r_m = sb("r_m", [P, NT])
        r_l = sb("r_l", [P, NT, NG])
        r_e = sb("r_e", [P, NT, NG])
        r_s = sb("r_s", [P, NT])
        r_r = sb("r_r", [P, NT])
        r_p = sb("r_p", [P, NT, NG])
        r_p2 = sb("r_p2", [P, NT, NG])
        r_q = sb("r_q", [P, NT, NG])
        r_k = sb("r_k", [P, NT, NG])
        oh = sb("oh", [P, NT, 2, NE], BF16)
        oh1 = sb("oh1", [P, NT, 2, NG])
        r_c = sb("r_c", [P, NT, 2, NE])
        prio = sb("prio", [P, NT, NE])
        Dm = sb("Dm", [P, NT, NE, CAP], BF16)
        Cm = shared[:].rearrange("p (n e c) -> p n e c", n=2, e=NE)
        CT = sb("CT", [P, NT, NE // 2, P])
        ein = sb("ein", [P, NE, 2, CAP])
        hT = [sb(f"hT{n}", [P, FC, 2, CAP]) for n in range(4)]
        eo = W[:].rearrange("p (k g) d -> p k g d", g=2)
        cw = sb("cw", [P, NT, NE])
        cwT = sb("cwT", [NT * NE, P])
        weighed = hT[0][:].rearrange("p c g s -> p (c g s)").rearrange("p (k e d) -> p k e d", k=2, e=2)
        pairs = hT[1][:].rearrange("p c g s -> p (c g s)")[:, 0:2 * D].rearrange("p (e d) -> p e d", e=2)
        acc = sb("acc", [P, NT, D])
        xres = acc
        bvb = a_xn[:, 0:LAYERS, :]

        SP3 = bank("SP3", [P, 3, 512])
        TB = [bank(f"TB{n}", [P, 512]) for n in range(2)]
        MB = bank("MB", [P, 512])
        HBK = bank("HBK", [P, 512])
        EBK = bank("EBK", [P, 512])

        names = """ld_ctx ld_x0 ld_x ld_w ld_col ld_gw ld_vec ld_moe ld_am ld_e1 st_out
        c_set c_ok c_idn k_ctxT k_ctxTs k_w k_ws k_kT k_kTs k_v k_vb k_kb k_pad k_gw k_gws
        a_stats a_aggr a_veps a_rstd a_xnok a_xTok a_xTs a_qok a_qTs a_xrok k_bvb k_bo k_bos k_idb k_kb1 a_vals
        biasok0 biasok1 maskn ampok
        scores added rowmax shifted probs trE PTs pv recips normed proj resid
        f_stats f_aggr f_veps f_rstd f_xnok f_xTok f_xTs
        m_logits m_route m_exp m_cum m_split m_D m_C m_disp m_eins m_CT m_CTs m_h m_hs m_eo m_eos m_comb m_out
        n_logits n_route n_exp n_cwT n_cwTs n_bias n_eo n_used n_acc n_sum n_scaled n_pair n_done""".split()
        s = {n: sem(n) for n in names}

        def value_banks(b):
            return (HBK, EBK) if b % 2 else (TB[0], TB[1])

        def static_first(run):
            return isinstance(run, int) and run == 0

        def wait_alone(eng, *waits):
            held = [(q, v if isinstance(v, int) else eng.to_reg(v)) for q, v in waits]
            eng.wait_ge(s["c_idn"], 1)
            for q, v in held:
                eng.wait_ge(q, v)

        def sl(t, run):
            return t[:, bass.ds(run, 1)]

        x_v = x.rearrange("b (g p r) d -> b p g r d", g=2, r=2)
        out_v = out.rearrange("b (g p r) d -> b p g r d", g=2, r=2)
        am_v = attn_mask.rearrange("(g p r) j -> p g r j", g=2, r=2)
        bias_v = bias.rearrange("b h (g p r) j -> b g p h (r j)", g=2, r=2)
        mask_v = mask.rearrange("b (g p r) j -> b g p (r j)", g=2, r=2)

        block = ctx.enter_context(nc.Block())

        @block.sync
        def _(sp):
            sp.dma_start(ctxn[:], ctx_in.rearrange("b j d -> j b d")).then_inc(s["ld_ctx"], 16)
            for n in range(4):
                sp.dma_start(W[:, n, :], w0[n]).then_inc(s["ld_w"], 16)
            for n in range(4):
                sp.dma_start(W[:, 4 + n, :], w1[n]).then_inc(s["ld_w"], 16)
            for n, v in enumerate((b0[0], b0[1], b0[2], b1[0], b1[1], b1[2])):
                sp.dma_start(bcol[:, n:n + 1], v.rearrange("(p o) -> p o", o=1)).then_inc(s["ld_col"], 16)
            for b in range(B):
                sp.dma_start(X[:, b].rearrange("p (g r) d -> p g r d", g=2), x_v[b])\
                    .then_inc(s["ld_x" if b else "ld_x0"], 16)
            for n, v in enumerate((b0[3], b1[3])):
                sp.dma_start(bo[:, n, :], v.partition_broadcast(P)).then_inc(s["ld_col"], 16)
            sp.dma_start(gw_s[:], gate_w).then_inc(s["ld_gw"], 16)

            def load_bias(a):
                for g, ok in enumerate(("biasok0", "biasok1")):
                    if not static_first(a):
                        wait_alone(sp, (s["added"], (a - 1) * 2 * NT + 4 * (g + 1)),
                                   (s["maskn"], (a - 1) * 2 + g + 1))
                    src_b = bias_v[bass.ds(a, 1), g].rearrange("o p h rj -> (o p) h rj")
                    src_m = mask_v[bass.ds(a, 1), g].rearrange("o p rj -> (o p) rj")
                    sp.dma_start(BI[g][:].rearrange("p h r j -> p h (r j)"), src_b).then_inc(s[ok], 16)
                    sp.dma_start(MI[g][:].rearrange("p r j -> p (r j)"), src_m).then_inc(s[ok], 16)

            load_bias(0)
            sp.dma_start(wi_s[:], wi.rearrange("e d f -> d e f")).then_inc(s["ld_moe"], 16)
            sp.dma_start(wo_s[:], wo.rearrange("e (c f) d -> f e c d", c=FC)).then_inc(s["ld_moe"], 16)
            sp.dma_start(wr_s[:], w_router).then_inc(s["ld_moe"], 16)
            sp.dma_start(am[:].rearrange("p (g r) j -> p g r j", g=2), am_v).then_inc(s["ld_am"], 16)
            sp.dma_start(padw[:], pad_mask.partition_broadcast(P)).then_inc(s["ld_am"], 16)
            sp.dma_start(ew_s[:], expert_w.rearrange("e d h -> d e h")).then_inc(s["ld_e1"], 16)
            with sp.Fori(1, B) as a:
                load_bias(a)

            def store(f):
                b = f - B
                wait_alone(sp, (s["n_done"], 1 + NT * (b + 1)))
                sp.dma_start(out_v[bass.ds(b, 1)].rearrange("o p g r d -> (o p) g r d"),
                             acc[:].rearrange("p (g r) d -> p g r d", g=2)).then_inc(s["st_out"], 16)

            store(B)
            with sp.Fori(1, B) as f:
                store(f + B)
            sp.wait_ge(s["st_out"], 16 * B)

        @block.gpsimd
        def _(pool):
            g = nc.gpsimd
            g.memset(ident[:], 0.0).then_inc(s["c_set"], 1)
            g.memset(headmask[:], 1.0).then_inc(s["n_done"], 1)
            pool.wait_ge(s["c_set"], 1)
            g.affine_select(out=ident[:], in_=ident[:], compare_op=ALU.not_equal, fill=1.0, base=0,
                            pattern=[[-1, P]], channel_multiplier=1).then_inc(s["c_idn"], 1)
            n_set = 1
            for t, v in ((rowmask, 1.0), (ones, 1.0), (incl, 1.0), (strict, 1.0),
                         (half, -0.5), (eb_s, 0.0), (identb, 0.0), (SC[0], 0.0), (SC[1], 0.0)):
                g.memset(t[:], v).then_inc(s["c_set"], 1)
                n_set += 1
            g.iota(iota1[:], pattern=[[1, CAP]], base=1, channel_multiplier=0,
                   allow_small_or_imprecise_dtypes=True).then_inc(s["c_ok"], 1)
            g.iota(rank[:], pattern=[[-1, NG]], base=NG, channel_multiplier=0,
                   allow_small_or_imprecise_dtypes=True).then_inc(s["c_ok"], 1)
            pool.wait_ge(s["c_set"], n_set)
            g.affine_select(out=headmask[:], in_=headmask[:], compare_op=ALU.is_ge, fill=0.0, base=0,
                            pattern=[[-DK, H]], channel_multiplier=1).then_inc(s["c_ok"], 1)
            pool.wait_ge(s["c_ok"], 3)
            g.affine_select(out=headmask[:], in_=headmask[:], compare_op=ALU.is_ge, fill=0.0, base=DK - 1,
                            pattern=[[DK, H]], channel_multiplier=-1).then_inc(s["c_ok"], 1)
            g.affine_select(out=incl[:], in_=incl[:], compare_op=ALU.is_ge, fill=0.0, base=0,
                            pattern=[[1, P]], channel_multiplier=-1).then_inc(s["c_ok"], 1)
            g.affine_select(out=strict[:], in_=strict[:], compare_op=ALU.is_ge, fill=0.0, base=-1,
                            pattern=[[1, P]], channel_multiplier=-1).then_inc(s["c_ok"], 1)
            QB = [[k for k in range(NB) if BLOCKS[k][0] == q] for q in range(4)]
            for q in range(4):
                k0, nq, base = QB[q][0], len(QB[q]), P * BLOCKS[QB[q][0]][1] - J * HQ * q
                part = rowmask[:, k0:k0 + nq]
                g.affine_select(out=part, in_=part, compare_op=ALU.is_ge, fill=0.0, base=base,
                                pattern=[[P, nq], [-J, HQ], [0, DK]], channel_multiplier=1).then_inc(s["c_ok"], 1)
            pool.wait_ge(s["c_ok"], 10)
            for q in range(4):
                k0, nq, base = QB[q][0], len(QB[q]), P * BLOCKS[QB[q][0]][1] - J * HQ * q
                part = rowmask[:, k0:k0 + nq]
                g.affine_select(out=part, in_=part, compare_op=ALU.is_ge, fill=0.0, base=J - 1 - base,
                                pattern=[[-P, nq], [J, HQ], [0, DK]], channel_multiplier=-1).then_inc(s["c_ok"], 1)
            g.affine_select(out=identb[:], in_=identb[:], compare_op=ALU.not_equal, fill=1.0, base=0,
                            pattern=[[-1, P]], channel_multiplier=1).then_inc(s["k_idb"], 1)

            g.dma_start(gb_s[:], gate_b.partition_broadcast(P)).then_inc(s["ld_vec"], 16)
            for i in range(NT):
                g.dma_start(eb_s[NE * i:NE * (i + 1), i, :], expert_b).then_inc(s["ld_vec"], 16)

            def rstd(aggr, mv, ve, rs, okv, okr, run):
                wait_alone(pool, (s[aggr], NT * (run + 1)))
                g.tensor_scalar(ve[:], mv[:, :, 1], EPS, None, ALU.add).then_inc(s[okv], 1)
                pool.wait_ge(s[okv], run + 1)
                g.tensor_tensor(rs[:], ve[:], half[:], ALU.pow).then_inc(s[okr], 1)

            def a_rstd(a):
                rstd("a_aggr", a_mv, a_ve, a_rs, "a_veps", "a_rstd", a)

            def f_rstd(f):
                rstd("f_aggr", f_mv, f_ve, f_rs, "f_veps", "f_rstd", f)

            def residual_bias(a, layer):
                if layer == 0:
                    if static_first(a):
                        pool.wait_ge(s["ld_x0"], 16)
                        pool.wait_ge(s["k_bos"], LAYERS)
                    else:
                        pool.wait_ge(s["ld_x"], 16 * (B - 1))
                else:
                    pool.wait_ge(s["m_out"], a - B + 2)
                if not static_first(a):
                    pool.wait_ge(s["resid"], NT * a)
                xin = sl(X, a - B * layer).rearrange("p o i d -> p (o i) d")
                g.tensor_tensor(xr[:], xin, bo[:, layer:layer + 1, :].broadcast_to([P, NT, D]),
                                ALU.add).then_inc(s["a_xrok"], 1)

            def mask_out(a, gi):
                wait_alone(pool, (s[f"biasok{gi}"], 32 * (a + 1)),
                           *([] if static_first(a) else [(s["scores"], 2 * NT * a)]))
                g.tensor_scalar(MN[gi][:], MI[gi][:], 0, MASKED, ALU.is_equal, ALU.mult)\
                    .then_inc(s["maskn"], 1)

            def block_keys(b, layer, done):
                g.tensor_tensor(sl(KB, b + B * layer).rearrange("p o (h j) -> p (o h) j", h=H),
                                kT[:, layer, bass.ds(b, 1), :].broadcast_to([P, H, J]),
                                headmask[:].unsqueeze(2).broadcast_to([P, H, J]), ALU.mult).then_inc(s[done], 1)

            def take_values(a):
                if static_first(a):
                    pool.wait_ge(s["k_vb"], 2 * B)
                else:
                    pool.wait_ge(s["pv"], NT * a)
                g.tensor_tensor(vals[:], sl(VB, a).rearrange("p o k (h d) -> p (o k) h d", h=HQ), rowmask[:],
                                ALU.mult).then_inc(s["a_vals"], 1)

            def shift(a, i):
                pool.wait_ge(s["rowmax"], NT * a + i + 1)
                S3 = SC[i % 2][:, 0:HJ].rearrange("p (h j) -> p h j", h=H)
                g.tensor_tensor(S3, S3, mx[i % 2][:].unsqueeze(2).broadcast_to([P, H, J]), ALU.subtract)\
                    .then_inc(s["shifted"], 1)

            def mask_attn(a):
                b = a - B
                if not static_first(b):
                    pool.wait_ge(s["added"], 2 * NT * a)
                g.tensor_tensor(amp[:], am[:], sl(padn, b).broadcast_to([P, NT, J]), ALU.add)\
                    .then_inc(s["ampok"], 1)

            def split_x(f):
                wait_alone(pool, (s["f_xnok"], NT * (f + 1)), *([] if static_first(f) else [(s["m_disp"], 2 * f)]))
                base = 4 * f
                g.tensor_copy(xh[:], f_xn[:]).then_inc(s["m_split"], 1)
                pool.wait_ge(s["m_split"], base + 1)
                g.tensor_tensor(xres[:], f_xn[:], xh[:], ALU.subtract).then_inc(s["m_split"], 1)
                wait_alone(pool, (s["m_split"], base + 2))
                g.tensor_copy(xm[:], xres[:]).then_inc(s["m_split"], 1)
                pool.wait_ge(s["m_split"], base + 3)
                g.tensor_tensor(xl[:], xres[:], xm[:], ALU.subtract).then_inc(s["m_split"], 1)

            def sum_experts(f, i):
                n = NT * (f - B) + i
                pool.wait_ge(s["n_scaled"], n + 1)
                if i > 0 or not static_first(f - B):
                    pool.wait_ge(s["n_done"], n + 1)
                g.tensor_tensor(pairs, weighed[:, 0], weighed[:, 1], ALU.add).then_inc(s["n_pair"], 1)
                pool.wait_ge(s["n_pair"], 2 * n + 1)
                g.tensor_tensor(pairs[:, 0, :], pairs[:, 0, :], pairs[:, 1, :], ALU.add).then_inc(s["n_pair"], 1)
                pool.wait_ge(s["n_pair"], 2 * n + 2)
                pool.wait_ge(s["n_used"], n + 1)
                g.tensor_tensor(acc[:, i, :], acc[:, i, :], pairs[:, 0, :], ALU.add).then_inc(s["n_done"], 1)

            def combine_weights(f, i):
                if static_first(f) and i == 0:
                    pool.wait_ge(s["k_v"], B)
                pool.wait_ge(s["m_D"], 2 * f + i // 2 + 1)
                if i >= 2 or not static_first(f):
                    pool.wait_ge(s["m_CT"], NT * f + i - 1)
                g.tensor_tensor(Cm[:, i % 2], Dm[:, i],
                                r_p[:, i, 0:NE].unsqueeze(2).broadcast_to([P, NE, CAP]),
                                ALU.mult).then_inc(s["m_C"], 1)

            def stretch(a, la, f, lf, m, lm):
                begins, ends = la is not None, lf is not None
                if begins:
                    a_rstd(a)
                if ends:
                    shift(f, 3)
                if la == 0:
                    mask_out(a, 0)
                if lm == 0:
                    combine_weights(m, 2)
                    combine_weights(m, 3)
                if lm == 1:
                    sum_experts(m, 0)
                if la == 1:
                    mask_attn(a)
                if la == 0:
                    block_keys(a, 0, "k_kb")
                if lm == 1:
                    sum_experts(m, 1)
                if la == 0:
                    mask_out(a, 1)
                if begins:
                    shift(a, 0)
                if ends:
                    f_rstd(f)
                if lm == 1:
                    sum_experts(m, 2)
                if begins:
                    take_values(a)
                    residual_bias(a, la)
                if lf == 0:
                    block_keys(f, 1, "k_kb1")
                if lm == 1:
                    sum_experts(m, 3)
                if begins:
                    shift(a, 1)
                if lf == 0:
                    split_x(f)
                    combine_weights(f, 0)
                    combine_weights(f, 1)
                if begins:
                    shift(a, 2)

            pool.wait_ge(s["k_kTs"], 2)
            pool.wait_ge(s["c_ok"], 14)
            stretch(0, 0, None, None, None, None)
            stretch(1, 0, 0, 0, None, None)
            with pool.Fori(2, B) as a:
                stretch(a, 0, a - 1, 0, a - 2, 0)
            pool.wait_ge(s["ld_am"], 32)
            g.tensor_scalar(padn[:], padb, -3e38, 2.0, ALU.mult, ALU.mult).then_inc(s["k_pad"], 1)
            pool.wait_ge(s["k_pad"], 1)
            stretch(B, 1, B - 1, 0, B - 2, 0)
            stretch(B + 1, 1, B, 1, B - 1, 0)
            with pool.Fori(B + 2, 2 * B) as a:
                stretch(a, 1, a - 1, 1, a - 2, 1)
            stretch(None, None, 2 * B - 1, 1, 2 * B - 2, 1)
            stretch(None, None, None, None, 2 * B - 1, 1)

        @block.scalar
        def _(act):
            sc = nc.scalar
            act.wait_ge(s["k_ctxT"], 1)
            for n in range(3):
                sc.copy(ctx3[:, :, n, :], MB[:, 0:B * J].rearrange("p (b j) -> p b j", b=B)).then_inc(s["k_ctxTs"], 1)
            for n in range(2):
                act.wait_ge(s["k_w"], n + 1)
                sc.copy(WT[:, 4 * n:4 * n + 4, :].rearrange("p n d -> p (n d)"), [HBK, EBK][n][:])\
                    .then_inc(s["k_ws"], 1)
            act.wait_ge(s["ld_col"], 16 * 8)
            for n in range(2):
                act.wait_ge(s["k_kT"], n + 1)
                sc.activation(kT[:, n].rearrange("p b j -> p (b j)"), SP3[:, n, 0:B * J], ACT.Identity,
                              bias=bcol[:, 3 * n + 1:3 * n + 2]).then_inc(s["k_kTs"], 1)
            act.wait_ge(s["k_gw"], 1)
            sc.copy(gwT[:], SP3[:, 2, 0:NG]).then_inc(s["k_gws"], 1)

            def a_xTcopy(a):
                act.wait_ge(s["a_xTok"], a + 1)
                sc.copy(a_xT[:], MB[:]).then_inc(s["a_xTs"], 1)

            def f_xTcopy(f):
                act.wait_ge(s["f_xTok"], f + 1)
                sc.copy(f_xT[:], MB[:]).then_inc(s["f_xTs"], 1)

            def softmax_exp(a, i):
                act.wait_ge(s["shifted"], NT * a + i + 1)
                sc.activation(SC[i % 2][:, 0:HJ], SC[i % 2][:, 0:HJ], ACT.Exp).then_inc(s["probs"], 1)

            def copy_PT(a, i, part):
                t = NT * a + i
                for n, (c0, c1) in (((0, (0, 4)), (1, (4, 8))), ((2, (8, NC)),))[part]:
                    act.wait_ge(s["trE"], 3 * t + n + 1)
                    if n == 0 and not static_first(a if i == 0 else 1):
                        act.wait_ge(s["pv"], t)
                    sc.copy(PT[:, c0:c1, :].rearrange("p c t -> p (c t)"),
                            TB[n % 2][:, 0:(c1 - c0) * P]).then_inc(s["PTs"], 1)

            def route_exp(route, per, k, ok, ne, run):
                act.wait_ge(s[route], per * run + k)
                sc.activation(r_e[:, :, 0:ne], r_l[:, :, 0:ne], ACT.Exp).then_inc(s[ok], 1)

            def copy_ein(f, g):
                act.wait_ge(s["m_disp"], 2 * f + g + 1)
                sc.copy(ein[:, :, g, :], [HBK, EBK][g][:].rearrange("p (e c) -> p e c", e=NE))\
                    .then_inc(s["m_eins"], 1)

            def copy_CT(f, i):
                act.wait_ge(s["m_CT"], NT * f + i + 1)
                sc.copy(CT[:, i].rearrange("p k t -> p (k t)"), [HBK, EBK][i % 2][:]).then_inc(s["m_CTs"], 1)

            def gelu(f, e):
                act.wait_ge(s["m_h"], NE * f + e + 1)
                sc.activation(hT[e % 4][:].rearrange("p c g s -> p (c g s)"), HBK[:], ACT.Gelu_apprx_tanh)\
                    .then_inc(s["m_hs"], 1)

            def copy_eo(f, k):
                act.wait_ge(s["m_eo"], NE // 2 * f + k + 1)
                sc.copy(eo[:, k].rearrange("p g d -> p (g d)"), EBK[:, 0:2 * D]).then_inc(s["m_eos"], 1)

            def scale_experts(f, i):
                n = NT * (f - B) + i
                act.wait_ge(s["n_eo"], 2 * n + 2)
                act.wait_ge(s["n_done"], n + 1)
                for e in range(NE // 2):
                    ins = sc.activation(weighed[:, e // 2, e % 2, :], EBK[:, e * D:(e + 1) * D], ACT.Identity,
                                        scale=cw[:, i, NE // 2 + e:NE // 2 + e + 1])
                ins.then_inc(s["n_scaled"], 1)

            def copy_cwT(f):
                act.wait_ge(s["n_cwT"], f - B + 1)
                sc.copy(cwT[:], EBK[0:NT * NE, 0:P]).then_inc(s["n_cwTs"], 1)

            def stretch(a, la, f, lf, m, lm):
                begins, ends = la is not None, lf is not None
                if lm == 0:
                    copy_ein(m, 0)
                if ends:
                    copy_PT(f, 2, 0)
                    copy_PT(f, 2, 1)
                if lm == 0:
                    copy_ein(m, 1)
                if lm == 1:
                    scale_experts(m, 0)
                if lm == 0:
                    copy_CT(m, 0)
                if ends:
                    softmax_exp(f, 3)
                if lm == 0:
                    copy_CT(m, 1)
                    copy_CT(m, 2)
                if lm == 1:
                    scale_experts(m, 1)
                if begins:
                    a_xTcopy(a)
                if lm == 0:
                    copy_CT(m, 3)
                if ends:
                    copy_PT(f, 3, 0)
                if lm == 0:
                    gelu(m, 0)
                if ends:
                    copy_PT(f, 3, 1)
                if lm == 0:
                    gelu(m, 1)
                if lm == 1:
                    scale_experts(m, 2)
                if lm == 0:
                    gelu(m, 2)
                    copy_eo(m, 0)
                    gelu(m, 3)
                if begins:
                    softmax_exp(a, 0)
                if lm == 0:
                    gelu(m, 4)
                    copy_eo(m, 1)
                if ends:
                    f_xTcopy(f)
                if lm == 1:
                    scale_experts(m, 3)
                if begins:
                    copy_PT(a, 0, 0)
                if lm == 0:
                    gelu(m, 5)
                if lf == 1:
                    route_exp("n_route", ROUTE1, 3, "n_exp", NG, f - B)
                if lf == 0:
                    route_exp("m_route", ROUTE0, 2, "m_exp", NE, f)
                if begins:
                    copy_PT(a, 0, 1)
                    softmax_exp(a, 1)
                if lm == 0:
                    gelu(m, 6)
                    copy_eo(m, 2)
                    gelu(m, 7)
                if begins:
                    copy_PT(a, 1, 0)
                    copy_PT(a, 1, 1)
                if lm == 0:
                    copy_eo(m, 3)
                if lf == 1:
                    copy_cwT(f)
                if begins:
                    softmax_exp(a, 2)

            stretch(0, 0, None, None, None, None)
            stretch(1, 0, 0, 0, None, None)
            with act.Fori(2, B) as a:
                stretch(a, 0, a - 1, 0, a - 2, 0)
            stretch(B, 1, B - 1, 0, B - 2, 0)
            stretch(B + 1, 1, B, 1, B - 1, 0)
            with act.Fori(B + 2, 2 * B) as a:
                stretch(a, 1, a - 1, 1, a - 2, 1)
            stretch(None, None, 2 * B - 1, 1, 2 * B - 2, 1)
            stretch(None, None, None, None, 2 * B - 1, 1)

        @block.tensor
        def _(pe):
            te = nc.tensor
            pe.wait_ge(s["c_idn"], 1)
            pe.wait_ge(s["ld_ctx"], 16)
            for b in range(B):
                last = te.transpose(MB[:, b * J:(b + 1) * J], ctxn[:, b, :], ident[0:J, 0:J])
            last.then_inc(s["k_ctxT"], 1)
            pe.wait_ge(s["ld_w"], 16 * 8)
            for n in range(8):
                last = te.transpose([HBK, EBK][n // 4][:, (n % 4) * D:(n % 4 + 1) * D], W[:, n, :], ident[:])
                if n % 4 == 3:
                    last.then_inc(s["k_w"], 1)
            pe.wait_ge(s["k_ctxTs"], 3)
            pe.wait_ge(s["k_ws"], 2)
            for n in range(2):
                te.matmul(SP3[:, n, 0:B * J], WT[:, 4 * n + 1, :], ctx3[:, :, 0, :],
                          start=True, stop=True).then_inc(s["k_kT"], 1)
            def values(b):
                if b >= 2:
                    pe.wait_ge(s["k_vb"], 2 * (b - 1))
                wv = WT[:].rearrange("p (l m) d -> p l m d", l=LAYERS)[:, :, 2, :]
                keys = ctx3[:, b].rearrange("p n j -> p (n j)")
                for c in range(NC):
                    ks = [k for k in range(NB) if BLOCKS[k][1] == c]
                    n, k0, q0 = ks[0] // VSPLIT, ks[0] % VSPLIT, BLOCKS[ks[0]][0]
                    o = value_banks(b)[n][:, 64 * k0:64 * (k0 + len(ks))].rearrange("p (k l x) -> p l k x",
                                                                                    l=LAYERS, x=32)
                    j0 = P * c % J
                    last = te.matmul(o, keys[:, j0:j0 + P],
                                     wv[:, :, 32 * q0:32 * (q0 + len(ks))].rearrange("p l (k x) -> p l k x", x=32),
                                     start=True, stop=True)
                last.then_inc(s["k_v"], 1)

            values(0)
            values(1)
            pe.wait_ge(s["k_bvb"], LAYERS)
            for n in range(LAYERS):
                te.matmul(MB[:, n * D:(n + 1) * D], bvb[:, n, :], WT[:, 4 * n + 3, :], start=True, stop=True)\
                    .then_inc(s["k_bo"], 1)
            values(2)
            values(3)
            pe.wait_ge(s["ld_gw"], 16)
            te.transpose(SP3[:, 2, 0:NG], gw_s[:], ident[0:NG, 0:NG]).then_inc(s["k_gw"], 1)
            pe.wait_ge(s["k_vb"], 2 * B)
            pe.wait_ge(s["k_bos"], LAYERS)
            pe.wait_ge(s["k_idb"], 1)

            def a_xTr(a):
                for i in range(NT):
                    pe.wait_ge(s["a_xnok"], NT * a + i + 1)
                    if i == 0 and not static_first(a):
                        pe.wait_ge(s["resid"], NT * a - 1)
                    last = te.transpose(MB[:, i * P:(i + 1) * P], a_xn[:, i, :], ident[:])
                last.then_inc(s["a_xTok"], 1)

            def query(a, layer):
                pe.wait_ge(s["a_xTs"], a + 1)
                te.matmul(MB[:], WT[:, 4 * layer, :], a_xT[:], start=True, stop=True).then_inc(s["a_qok"], 1)

            def attn_scores(a, i, layer):
                t = NT * a + i
                g, r = i // 2, i % 2
                if i == 0:
                    pe.wait_ge(s["a_qTs"], a + 1)
                    if layer == 0:
                        pe.wait_ge(s["k_kb"], a + 1)
                    else:
                        pe.wait_ge(s["k_kb1"], a - B + 1)
                if layer == 0 and r == 0:
                    pe.wait_ge(s["maskn"], 2 * a + g + 1)
                kb = sl(KB, a).rearrange("p o n -> p (o n)")
                for n, (h0, h1) in enumerate(BANKS):
                    if n != 1 and not static_first(a if i == 0 else 1):
                        pe.wait_ge(s["added"], 2 * (t - 1) + (1 if n == 0 else 2))
                    last = te.matmul(SP3[:, n, 0:(h1 - h0) * J], qT[:, i * P:(i + 1) * P],
                                     kb[:, h0 * J:h1 * J], start=True, stop=(layer == 1))
                    if layer == 0:
                        last = te.matmul(SP3[:, n, 0:(h1 - h0) * J], identb[:],
                                         MN[g][:, r:r + 1, :].broadcast_to([P, h1 - h0, J]),
                                         start=False, stop=True)
                    if n > 0:
                        last.then_inc(s["scores"], 1)

            def turn_probs(a, i, n, c0, c1):
                t = NT * a + i
                if n == 0:
                    pe.wait_ge(s["probs"], t + 1)
                if n == 0 and not static_first(a if i == 0 else 1):
                    pe.wait_ge(s["PTs"], 3 * t)
                if n == 2:
                    pe.wait_ge(s["PTs"], 3 * t + 1)
                for c in range(c0, c1):
                    last = te.transpose(TB[n % 2][:, (c - c0) * P:(c - c0 + 1) * P],
                                        SC[i % 2][:, c * P:(c + 1) * P], ident[:])
                last.then_inc(s["trE"], 1)

            def weigh_values(a, i):
                t = NT * a + i
                if i == 0:
                    pe.wait_ge(s["a_vals"], a + 1)
                else:
                    pe.wait_ge(s["resid"], NT * a + i)
                pe.wait_ge(s["PTs"], 3 * t + 3)
                for m in range(2):
                    for n, ks in enumerate(ROUNDS):
                        for k in ks:
                            q, c = BLOCKS[k]
                            mine = [j for j in range(NB) if BLOCKS[j][0] == q]
                            w = (vals, rowmask)[m][:, k].rearrange("p h d -> p (h d)")
                            last = te.matmul(MB[32 * q:32 * (q + 1), m * P:(m + 1) * P], w, PT[:, c, :],
                                             start=(k == mine[0]), stop=(k == mine[-1]))
                last.then_inc(s["pv"], 1)

            def project(a, i, layer):
                pe.wait_ge(s["normed"], NT * a + i + 1)
                te.matmul(MB[:, 2 * P:2 * P + D], oT[:], WT[:, 4 * layer + 3, :], start=True, stop=True)\
                    .then_inc(s["proj"], 1)

            def turn(a, i, part):
                if part == 0:
                    turn_probs(a, i, 0, 0, 4)
                    turn_probs(a, i, 1, 4, 8)
                else:
                    turn_probs(a, i, 2, 8, NC)

            def f_xTr(f):
                for i in range(NT):
                    pe.wait_ge(s["f_xnok"], NT * f + i + 1)
                    last = te.transpose(MB[:, i * P:(i + 1) * P], f_xn[:, i, :], ident[:])
                last.then_inc(s["f_xTok"], 1)

            def logits0(f):
                pe.wait_ge(s["f_xTs"], f + 1)
                if static_first(f):
                    pe.wait_ge(s["ld_moe"], 48)
                for i in range(NT):
                    last = te.matmul(MB[:, i * NE:(i + 1) * NE], f_xT[:, i * P:(i + 1) * P], wr_s[:],
                                     start=True, stop=True)
                last.then_inc(s["m_logits"], 1)

            def positions(f):
                pe.wait_ge(s["m_route"], ROUTE0 * f + 16)
                if not static_first(f):
                    pe.wait_ge(s["m_eos"], NE // 2 * f - 1)
                for g in range(2):
                    t0, t1 = 2 * g, 2 * g + 1
                    for i, first in ((t0, incl), (t1, incl)):
                        o = EBK[:, 2 * P + i * 2 * NE:2 * P + (i + 1) * 2 * NE]
                        second = strict if i == t0 else incl
                        te.matmul(o, first[:], oh[:, t0].rearrange("p k e -> p (k e)"),
                                  start=True, stop=False, skip_group_check=True)
                        te.matmul(o, second[:], oh[:, t1].rearrange("p k e -> p (k e)"),
                                  start=False, stop=False, skip_group_check=True)
                        te.matmul(o[:, NE:], ones[:], oh[:, t0, 0, :], start=False, stop=False,
                                  skip_group_check=True)
                        last = te.matmul(o[:, NE:], ones[:], oh[:, t1, 0, :], start=False, stop=True,
                                         skip_group_check=True)
                last.then_inc(s["m_cum"], 1)

            def dispatch(f, g):
                pe.wait_ge(s["m_split"], 4 * f + 4)
                if g == 0:
                    pe.wait_ge(s["m_out"], f + 1)
                pe.wait_ge(s["m_D"], 2 * f + g + 1)
                n = 0
                for i in (2 * g, 2 * g + 1):
                    for part in (xh, xm, xl):
                        last = te.matmul([HBK, EBK][g][:], part[:, i, :], Dm[:, i].rearrange("p e c -> p (e c)"),
                                         start=(n == 0), stop=(n == 5))
                        n += 1
                last.then_inc(s["m_disp"], 1)

            def turn_C(f, i):
                pe.wait_ge(s["m_C"], NT * f + i + 1)
                if i < 2:
                    pe.wait_ge(s["m_eins"], 2 * f + i + 1)
                else:
                    pe.wait_ge(s["m_CTs"], NT * f + i - 1)
                for k in range(NE // 2):
                    last = te.transpose([HBK, EBK][i % 2][:, k * P:(k + 1) * P],
                                        Cm[:, i % 2, 2 * k:2 * k + 2, :].rearrange("p e c -> p (e c)"), ident[:])
                last.then_inc(s["m_CT"], 1)

            def up(f, e):
                if e == 0:
                    pe.wait_ge(s["m_CTs"], NT * f + NT)
                else:
                    pe.wait_ge(s["m_hs"], NE * f + e)
                for c in range(FC):
                    last = te.matmul(HBK[:, c * P:(c + 1) * P], wi_s[:, e, c * P:(c + 1) * P],
                                     ein[:, e].rearrange("p g c -> p (g c)"), start=True, stop=True)
                last.then_inc(s["m_h"], 1)

            def down(f, k):
                pe.wait_ge(s["m_hs"], NE * f + 2 * k + 2)
                if k > 0:
                    pe.wait_ge(s["m_eos"], NE // 2 * f + k)
                for g in range(2):
                    for c in range(FC):
                        for q in range(2):
                            last = te.matmul(EBK[q * CAP:(q + 1) * CAP, g * D:(g + 1) * D], hT[(2 * k + q) % 4][:, c, g, :],
                                             wo_s[:, 2 * k + q, c, :], start=(c == 0), stop=(c == FC - 1))
                last.then_inc(s["m_eo"], 1)

            def combine(f, n):
                pe.wait_ge(s["m_eos"], NE // 2 * (f + 1))
                for i in (2 * n, 2 * n + 1):
                    for k in range(NE // 2):
                        last = te.matmul(HBK[:, i * D:(i + 1) * D], CT[:, i, k, :], eo[:, k, i // 2, :],
                                         start=(k == 0), stop=(k == NE // 2 - 1))
                if n == 1:
                    last.then_inc(s["m_comb"], 1)

            def logits1(f):
                pe.wait_ge(s["f_xTs"], f + 1)
                if static_first(f - B):
                    pe.wait_ge(s["k_gws"], 1)
                    pe.wait_ge(s["ld_e1"], 16)
                for i in range(NT):
                    last = te.matmul(MB[:, i * NG:(i + 1) * NG], f_xT[:, i * P:(i + 1) * P], gwT[:],
                                     start=True, stop=True)
                last.then_inc(s["n_logits"], 1)

            def expert_bias(f):
                m = f - B
                pe.wait_ge(s["n_route"], ROUTE1 * (m + 1))
                if static_first(m):
                    pe.wait_ge(s["m_eos"], NE // 2 * B)
                    pe.wait_ge(s["m_out"], B + 1)
                else:
                    pe.wait_ge(s["n_used"], NT * m)
                    pe.wait_ge(s["n_scaled"], NT * m)
                te.transpose(EBK[0:NT * NE, 0:P], cw[:].rearrange("p i e -> p (i e)"), ident[:])\
                    .then_inc(s["n_cwT"], 1)
                if static_first(m):
                    pe.wait_ge(s["ld_vec"], 16 * 5)
                pe.wait_ge(s["n_cwTs"], m + 1)
                te.matmul(EBK[:], cwT[:], eb_s[:].rearrange("k i d -> k (i d)"), start=True, stop=True)\
                    .then_inc(s["n_bias"], 1)

            def experts(f, i):
                m = f - B
                for n in range(2):
                    if i == 0:
                        pe.wait_ge(s["n_acc"], m + 1)
                    else:
                        pe.wait_ge(s[("n_used", "n_scaled")[n]], NT * m + i)
                    te.matmul([HBK, EBK][n][:], f_xT[:, i * P:(i + 1) * P],
                              ew_s[:, 4 * n:4 * n + 4, :].rearrange("p e d -> p (e d)"),
                              start=True, stop=True).then_inc(s["n_eo"], 1)

            def stretch(a, la, f, lf, m, lm):
                begins, ends = la is not None, lf is not None
                if ends:
                    attn_scores(f, 3, lf)
                    project(f, 1, lf)
                if lm == 0:
                    dispatch(m, 0)
                if ends:
                    turn(f, 2, 0)
                if lm == 0:
                    dispatch(m, 1)
                if ends:
                    turn(f, 2, 1)
                if lm == 0:
                    turn_C(m, 0)
                if lm == 1:
                    experts(m, 0)
                if ends:
                    weigh_values(f, 2)
                if lm == 0:
                    turn_C(m, 1)
                if lm == 1:
                    experts(m, 1)
                if lm == 0:
                    turn_C(m, 2)
                if ends:
                    project(f, 2, lf)
                if lm == 0:
                    turn_C(m, 3)
                if begins:
                    a_xTr(a)
                if ends:
                    turn(f, 3, 0)
                if begins:
                    query(a, la)
                if lm == 0:
                    up(m, 0)
                if ends:
                    turn(f, 3, 1)
                if lm == 1:
                    experts(m, 2)
                if begins:
                    attn_scores(a, 0, la)
                if lm == 0:
                    up(m, 1)
                if begins and ends:
                    pe.wait_ge(s["a_qTs"], a + 1)
                if ends:
                    weigh_values(f, 3)
                if lm == 0:
                    up(m, 2)
                if lm == 1:
                    experts(m, 3)
                if lm == 0:
                    down(m, 0)
                    up(m, 3)
                if ends:
                    project(f, 3, lf)
                if begins:
                    attn_scores(a, 1, la)
                if lm == 0:
                    up(m, 4)
                    down(m, 1)
                if ends:
                    f_xTr(f)
                if begins:
                    turn(a, 0, 0)
                if lm == 0:
                    up(m, 5)
                if lf == 0:
                    logits0(f)
                if lf == 1:
                    logits1(f)
                if begins:
                    turn(a, 0, 1)
                    attn_scores(a, 2, la)
                if lm == 0:
                    up(m, 6)
                    down(m, 2)
                if begins and lf == 0:
                    pe.wait_ge(s["m_route"], ROUTE0 * f + 2)
                if begins and lf == 1:
                    pe.wait_ge(s["n_route"], ROUTE1 * (f - B) + 1)
                if begins:
                    weigh_values(a, 0)
                if lm == 0:
                    up(m, 7)
                if begins:
                    turn(a, 1, 0)
                if lf == 0:
                    positions(f)
                if begins:
                    project(a, 0, la)
                    turn(a, 1, 1)
                if lm == 0 and lf == 0:
                    pe.wait_ge(s["m_route"], ROUTE0 * f + 17)
                if lm == 0:
                    down(m, 3)
                if begins:
                    weigh_values(a, 1)
                if lm == 0:
                    combine(m, 0)
                    combine(m, 1)
                if lf == 1:
                    expert_bias(f)

            stretch(0, 0, None, None, None, None)
            stretch(1, 0, 0, 0, None, None)
            with pe.Fori(2, B) as a:
                stretch(a, 0, a - 1, 0, a - 2, 0)
            stretch(B, 1, B - 1, 0, B - 2, 0)
            stretch(B + 1, 1, B, 1, B - 1, 0)
            with pe.Fori(B + 2, 2 * B) as a:
                stretch(a, 1, a - 1, 1, a - 2, 1)
            stretch(None, None, 2 * B - 1, 1, 2 * B - 2, 1)
            stretch(None, None, None, None, 2 * B - 1, 1)

        @block.vector
        def _(dve):
            v = nc.vector
            dve.wait_ge(s["ld_col"], 16 * 8)
            for n in range(LAYERS):
                v.tensor_copy(bvb[:, n, :], bcol[:, 3 * n + 2:3 * n + 3].broadcast_to([P, P])).then_inc(s["k_bvb"], 1)
            dve.wait_ge(s["c_ok"], 14)

            def mask_values(b):
                dve.wait_ge(s["k_v"], b + 1)
                for n, (k0, k1) in enumerate(((0, VSPLIT), (VSPLIT, NB))):
                    for l in range(LAYERS):
                        ins = v.tensor_tensor(
                            VB[:, b + l * B, k0:k1, :],
                            value_banks(b)[n][:, 0:64 * (k1 - k0)].rearrange("p (k l x) -> p l k x",
                                                                             l=LAYERS, x=32)[:, l],
                            rowmask[:, k0:k1].rearrange("p k h d -> p k (h d)"), ALU.mult)
                    ins.then_inc(s["k_vb"], 1)

            mask_values(0)
            mask_values(1)
            dve.wait_ge(s["k_bo"], LAYERS)
            for n in range(LAYERS):
                v.tensor_tensor(bo[:, n, :], bo[:, n, :], MB[:, n * D:(n + 1) * D], ALU.add).then_inc(s["k_bos"], 1)
            mask_values(2)
            mask_values(3)
            dve.wait_ge(s["k_vb"], 2 * B)
            v.memset(r_m[:], 0.0).then_inc(s["m_out"], 1)

            def x_of(run, layer):
                return sl(X, run - B * layer).rearrange("p o i d -> p (o i) d")

            def statistics(pre, st, mv, run, layer, i0, i1):
                for i in range(i0, i1):
                    v.bn_stats(st[:, i, :], x_of(run, layer)[:, i, :]).then_inc(s[pre + "_stats"], 1)

            def aggregate(pre, st, mv, run):
                for i in range(NT):
                    wait_alone(dve, (s[pre + "_stats"], NT * run + i + 1))
                    v.bn_aggr(mv[:, i, :], st[:, i, :]).then_inc(s[pre + "_aggr"], 1)

            def layer_norm(pre, mv, rs, xn, run, layer):
                if not static_first(run):
                    dve.wait_ge(s[pre + "_xTok"], run)
                    if pre == "f":
                        dve.wait_ge(s["m_split"], 4 * run if layer == 0 else 4 * B)
                dve.wait_ge(s[pre + "_rstd"], run + 1)
                for i in range(NT):
                    v.tensor_scalar(xn[:, i, :], x_of(run, layer)[:, i, :], mv[:, i, 0:1], rs[:, i:i + 1],
                                    ALU.subtract, ALU.mult).then_inc(s[pre + "_xnok"], 1)

            def a_stats(a, layer):
                if layer == 1:
                    wait_alone(dve, (s["m_out"], a - B + 2))
                elif static_first(a):
                    dve.wait_ge(s["ld_x0"], 16)
                else:
                    wait_alone(dve, (s["ld_x"], 16 * (B - 1)))
                statistics("a", a_st, a_mv, a, layer, 0, NT)
                aggregate("a", a_st, a_mv, a)

            def a_norm(a, layer):
                layer_norm("a", a_mv, a_rs, a_xn, a, layer)

            def f_stats(f, layer, i0, i1):
                wait_alone(dve, (s["resid"], NT * f + i1))
                statistics("f", f_st, f_mv, f, layer, i0, i1)
                if i1 == NT:
                    aggregate("f", f_st, f_mv, f)

            def f_norm(f, layer):
                layer_norm("f", f_mv, f_rs, f_xn, f, layer)

            def scale_q(a, layer):
                dve.wait_ge(s["a_qok"], a + 1)
                v.tensor_scalar(qT[:], MB[:], bcol[:, 3 * layer:3 * layer + 1], SCALE, ALU.add, ALU.mult)\
                    .then_inc(s["a_qTs"], 1)

            def softmax_max(a, i, layer):
                t = NT * a + i
                g, r = i // 2, i % 2
                S_ = SC[i % 2]
                if layer == 0 and r == 0:
                    dve.wait_ge(s[f"biasok{g}"], 32 * (a + 1))
                if layer == 1 and i == 0:
                    dve.wait_ge(s["ampok"], a - B + 1)
                if not static_first(a) or i >= 2:
                    dve.wait_ge(s["trE"], 3 * (t - 1))
                for n, (h0, h1, k) in enumerate(((0, 2 * HB, 2), (2 * HB, H, 1))):
                    dve.wait_ge(s["scores"], 2 * t + n + 1)
                    hh = (h1 - h0) // k
                    shape = [P, k, hh, J]
                    o = S_[:, h0 * J:h1 * J].rearrange("p (k h j) -> p k h j", k=k, h=hh)
                    i0 = SP3[:, 2 * n:2 * n + k, 0:hh * J].rearrange("p k (h j) -> p k h j", h=hh)
                    if layer == 0:
                        i1 = BI[g][:, h0:h1, r, :].rearrange("p (k h) j -> p k h j", k=k)
                    else:
                        i1 = amp[:, i:i + 1, :].unsqueeze(1).broadcast_to(shape)
                    v.tensor_tensor(o, i0, i1, ALU.add).then_inc(s["added"], 1)
                dve.wait_ge(s["added"], 2 * t + 2)
                S3 = S_[:, 0:HJ].rearrange("p (h j) -> p h j", h=H)
                v.tensor_reduce(mx[i % 2][:], S3, AX.X, ALU.max).then_inc(s["rowmax"], 1)

            def normalise(a, i):
                t = NT * a + i
                dve.wait_ge(s["pv"], t + 1)
                v.reciprocal(rc[:], MB[:, P:2 * P]).then_inc(s["recips"], 1)
                dve.wait_ge(s["recips"], t + 1)
                v.tensor_tensor(oT[:], MB[:, 0:P], rc[:], ALU.mult).then_inc(s["normed"], 1)

            def add_residual(a, i, layer):
                dve.wait_ge(s["proj"], NT * a + i + 1)
                if i == 0:
                    dve.wait_ge(s["a_xrok"], a + 1)
                xo = sl(X, a - B * layer).rearrange("p o i d -> p (o i) d")
                v.tensor_tensor(xo[:, i, :], MB[:, 2 * P:2 * P + D], xr[:, i, :], ALU.add).then_inc(s["resid"], 1)

            def top2_start(step, ne, lg):
                step(v.tensor_reduce(r_m[:], lg, AX.X, ALU.max))
                step(v.tensor_tensor(r_l[:, :, 0:ne], lg, r_m[:].unsqueeze(2).broadcast_to([P, NT, ne]), ALU.subtract))

            def top2(step, ne, o1, o2, exp_ok, run):
                nb = [P, NT, ne]
                e_, p_, p2, q_, k_ = (z[:, :, 0:ne] for z in (r_e, r_p, r_p2, r_q, r_k))
                rk = rank[:, 0:ne].unsqueeze(1).broadcast_to(nb)
                bc = lambda z: z[:].unsqueeze(2).broadcast_to(nb)
                dve.wait_ge(s[exp_ok], run + 1)
                step(v.tensor_reduce(r_s[:], e_, AX.X, ALU.add))
                step(v.reciprocal(r_r[:], r_s[:]))
                step(v.tensor_tensor(p_, e_, bc(r_r), ALU.mult))
                for n, (src, o) in enumerate(((p_, o1), (p2, o2))):
                    step(v.tensor_reduce(r_m[:], src, AX.X, ALU.max))
                    step(v.tensor_tensor(q_, src, bc(r_m), ALU.is_equal))
                    step(v.tensor_tensor(k_, q_, rk, ALU.mult))
                    step(v.tensor_reduce(r_s[:], k_, AX.X, ALU.max))
                    step(v.tensor_tensor(o, k_, bc(r_s), ALU.is_equal))
                    if n == 0:
                        step(v.scalar_tensor_tensor(p2, o, -2.0, p_, ALU.mult, ALU.add))

            class Steps:

                def __init__(self, name, base):
                    self.name, self.base, self.n = name, base, 0

                def __call__(self, ins):
                    self.n += 1
                    ins.then_inc(s[self.name], 1)
                    dve.wait_ge(s[self.name], self.base + self.n)

            def start0(f):
                dve.wait_ge(s["m_logits"], f + 1)
                top2_start(Steps("m_route", ROUTE0 * f), NE, MB[:, 0:NT * NE].rearrange("p (i e) -> p i e", i=NT))

            def route0(f):
                top2(Steps("m_route", ROUTE0 * f + 2), NE, oh[:, :, 0, :], oh[:, :, 1, :], "m_exp", f)

            def slots(f):
                st = Steps("m_route", ROUTE0 * f + ROUTE0 - 2)
                dve.wait_ge(s["m_cum"], f + 1)
                st(v.tensor_tensor(r_c[:].rearrange("p i k e -> p (i k e)"), EBK[:, 2 * P:2 * P + NT * 2 * NE],
                                   oh[:].rearrange("p i k e -> p (i k e)"), ALU.mult))
                st(v.tensor_tensor(prio[:], r_c[:, :, 0, :], r_c[:, :, 1, :], ALU.add))
                for g in range(2):
                    shape = [P, 2 * NE, CAP]
                    v.tensor_tensor(Dm[:, 2 * g:2 * g + 2].rearrange("p i e c -> p (i e) c"),
                                    iota1[:].unsqueeze(1).broadcast_to(shape),
                                    prio[:, 2 * g:2 * g + 2, :].rearrange("p i e -> p (i e)").unsqueeze(2)
                                    .broadcast_to(shape), ALU.is_equal).then_inc(s["m_D"], 1)

            def add_mixture(f):
                dve.wait_ge(s["m_comb"], f + 1)
                xo = sl(X, f).rearrange("p o i d -> p (o i d)")
                v.tensor_tensor(xo, xo, HBK[:], ALU.add).then_inc(s["m_out"], 1)

            def start1(f):
                m = f - B
                dve.wait_ge(s["n_logits"], m + 1)
                if static_first(m):
                    dve.wait_ge(s["ld_vec"], 16 * 5)
                st = Steps("n_route", ROUTE1 * m)
                st(v.tensor_tensor(r_p2[:], MB[:, 0:NT * NG].rearrange("p (i e) -> p i e", i=NT),
                                   gb_s[:].unsqueeze(1).broadcast_to([P, NT, NG]), ALU.add))
                top2_start(st, NG, r_p2[:])

            def route1(f):
                m = f - B
                st = Steps("n_route", ROUTE1 * m + 3)
                top2(st, NG, oh1[:, :, 0, :], oh1[:, :, 1, :], "n_exp", m)
                st(v.tensor_tensor(r_q[:], oh1[:, :, 0, :], oh1[:, :, 1, :], ALU.add))
                if not static_first(m):
                    dve.wait_ge(s["n_scaled"], NT * m)
                st(v.tensor_tensor(cw[:], r_p[:, :, 0:NE], r_q[:, :, 0:NE], ALU.mult))
                st(v.tensor_reduce(r_s[:], cw[:], AX.X, ALU.add))
                st(v.tensor_scalar(r_m[:], r_s[:], 0.0, None, ALU.is_le))
                st(v.tensor_tensor(r_s[:], r_s[:], r_m[:], ALU.add))
                st(v.reciprocal(r_r[:], r_s[:]))
                st(v.tensor_tensor(cw[:], cw[:], r_r[:].unsqueeze(2).broadcast_to([P, NT, NE]), ALU.mult))
                assert st.n == ROUTE1 - 3

            def start_acc(f):
                m = f - B
                dve.wait_ge(s["n_bias"], m + 1)
                xo = sl(X, m).rearrange("p o i d -> p (o i d)")
                if not static_first(m):
                    dve.wait_ge(s["st_out"], 16 * m)
                v.tensor_tensor(acc[:].rearrange("p i d -> p (i d)"), EBK[:], xo, ALU.add).then_inc(s["n_acc"], 1)
                dve.wait_ge(s["n_acc"], m + 1)

            def weigh_experts(f, i):
                n = NT * (f - B) + i
                dve.wait_ge(s["n_eo"], 2 * n + 1)
                for e in range(NE // 2):
                    ins = v.scalar_tensor_tensor(acc[:, i, :], HBK[:, e * D:(e + 1) * D],
                                                 cw[:, i, e:e + 1], acc[:, i, :], ALU.mult, ALU.add)
                    if e < NE // 2 - 1:
                        ins.then_inc(s["n_sum"], 1)
                        dve.wait_ge(s["n_sum"], 3 * n + e + 1)
                ins.then_inc(s["n_used"], 1)

            def stretch(a, la, f, lf, m, lm):
                begins, ends = la is not None, lf is not None
                if begins:
                    a_stats(a, la)
                if ends:
                    softmax_max(f, 3, lf)
                    add_residual(f, 1, lf)
                if lm == 1:
                    weigh_experts(m, 0)
                if begins:
                    a_norm(a, la)
                if ends:
                    normalise(f, 2)
                    add_residual(f, 2, lf)
                if lm == 1:
                    weigh_experts(m, 1)
                if begins:
                    scale_q(a, la)
                if lm == 1:
                    weigh_experts(m, 2)
                if begins:
                    softmax_max(a, 0, la)
                if ends:
                    normalise(f, 3)
                    f_stats(f, lf, 0, NT - 1)
                    add_residual(f, 3, lf)
                    f_stats(f, lf, NT - 1, NT)
                if lm == 1:
                    weigh_experts(m, 3)
                if ends:
                    f_norm(f, lf)
                if begins:
                    softmax_max(a, 1, la)
                if lf == 0:
                    start0(f)
                    route0(f)
                if lf == 1:
                    start1(f)
                    route1(f)
                if begins:
                    normalise(a, 0)
                    add_residual(a, 0, la)
                if lf == 0:
                    slots(f)
                if begins:
                    softmax_max(a, 2, la)
                    normalise(a, 1)
                if lm == 0:
                    add_mixture(m)
                if lf == 1:
                    start_acc(f)

            stretch(0, 0, None, None, None, None)
            stretch(1, 0, 0, 0, None, None)
            with dve.Fori(2, B) as a:
                stretch(a, 0, a - 1, 0, a - 2, 0)
            stretch(B, 1, B - 1, 0, B - 2, 0)
            stretch(B + 1, 1, B, 1, B - 1, 0)
            with dve.Fori(B + 2, 2 * B) as a:
                stretch(a, 1, a - 1, 1, a - 2, 1)
            stretch(None, None, 2 * B - 1, 1, 2 * B - 2, 1)
            stretch(None, None, None, None, 2 * B - 1, 1)


_INS = ['x', 'ctx_1024', 'fside_Bx16xSxS2_0', 'fside_SxS2_0', 'mask_BxSxS2_ik1', 'mask_BxS2_bf0',
        'L0_xattn_Wq', 'L0_xattn_bq', 'L0_xattn_Wk', 'L0_xattn_bk', 'L0_xattn_Wv', 'L0_xattn_bv',
        'L0_xattn_Wo', 'L0_xattn_bo', 'L0_ffn_w_router', 'L0_ffn_wi', 'L0_ffn_wo',
        'L1_xattn_Wq', 'L1_xattn_bq', 'L1_xattn_Wk', 'L1_xattn_bk', 'L1_xattn_Wv', 'L1_xattn_bv',
        'L1_xattn_Wo', 'L1_xattn_bo', 'L1_ffn_gate_w', 'L1_ffn_gate_b', 'L1_ffn_expert_w', 'L1_ffn_expert_b']


def kernel(**inputs):
    import numpy as _np
    import concourse.bacc as _bacc
    from concourse import mybir as _mybir
    from concourse.bass_utils import run_bass_kernel_spmd as _run

    nc = _bacc.Bacc("TRN2", target_bir_lowering=False, num_devices=1)
    arrays, t = {}, {}
    for name in _INS:
        a = _np.ascontiguousarray(inputs[name])
        if a.dtype == _np.bool_:
            a = a.reshape(-1).view(_np.int32)
        arrays[f"in_{name}"] = a
        t[name] = nc.dram_tensor(f"in_{name}", a.shape, _mybir.dt.from_np(a.dtype), kind="ExternalInput").ap()
    out = nc.dram_tensor("out", inputs["x"].shape, _mybir.dt.float32, kind="ExternalOutput").ap()
    heads = [[t[f"L{n}_xattn_{k}{m}"] for m in "qkvo"] for n in range(2) for k in "Wb"]
    bass_xattn_moe_twice(
        nc, t['x'], t['ctx_1024'], t['fside_Bx16xSxS2_0'], t['fside_SxS2_0'], t['mask_BxSxS2_ik1'],
        t['mask_BxS2_bf0'], heads[0], heads[1], t['L0_ffn_w_router'], t['L0_ffn_wi'], t['L0_ffn_wo'],
        heads[2], heads[3], t['L1_ffn_gate_w'], t['L1_ffn_gate_b'], t['L1_ffn_expert_w'],
        t['L1_ffn_expert_b'], out)
    r = _run(nc, [arrays], core_ids=[0])
    return r.results[0]["out"]
```
